# Optimizing a Trainium2 kernel written in Bass

```python
import numpy as np
import jax
import jax.numpy as jnp

def _softmax(x, axis=-1):
    return jax.nn.softmax(x, axis=axis)

def _gelu(x):
    return jax.nn.gelu(x, approximate=True)

def _silu(x):
    return jax.nn.silu(x)

def _sigmoid(x):
    return jax.nn.sigmoid(x)

def _layernorm(x, axis=-1, eps=1e-05):
    m = jnp.mean(x, axis=axis, keepdims=True)
    v = jnp.var(x, axis=axis, keepdims=True)
    return (x - m) / jnp.sqrt(v + eps)

def _scatter_add(tgt, idx, src, axis=0):
    return tgt.at[idx].add(src)

def _segment_sum(src, seg, n):
    return jax.ops.segment_sum(src, seg, n)
kernel_name = 'mk_flamingo_gated_d2_seqx_r8_879a4f'

def setup_inputs(seed: int=0):
    np.random.seed(seed)
    _w = jnp.asarray

    def _rec_inputs():
        import jax
        import jax.numpy as jnp
        _rk = jax.random.key(seed)
        x = -0.0003929 + 0.9999 * jax.random.normal(jax.random.fold_in(_rk, 1), (4, 512, 128), jnp.float32)
        _lenS = 512 - jax.random.randint(jax.random.fold_in(_rk, 7), (4,), 0, max(1, 512 // 4) + 1, jnp.int32)
        _lenS2 = 154 - jax.random.randint(jax.random.fold_in(_rk, 8), (4,), 0, max(1, 154 // 4) + 1, jnp.int32)
        _ctx_768P = jax.random.normal(jax.random.fold_in(_rk, 11), (4, 16, 96), jnp.float32)
        _ctx_768c = jax.random.dirichlet(jax.random.fold_in(_rk, 511), 0.3 * jnp.ones((16,), jnp.float32), (4, 154))
        _ctx_768t = jnp.einsum('bsk,bkd->bsd', _ctx_768c, _ctx_768P)
        _ctx_768t = _ctx_768t * jax.lax.rsqrt(jnp.mean(jnp.square(_ctx_768t)) + 1e-12) * 0.953939
        ctx_768 = -7.36909e-05 + 0.999899 * (_ctx_768t + 0.3 * jax.random.normal(jax.random.fold_in(_rk, 611), (4, 154, 96), jnp.float32))
        _g = jax.random.normal(jax.random.fold_in(_rk, 9001), (2, 2), jnp.float32)
        _g = jnp.sign(_g) * jnp.maximum(jnp.abs(_g), 1.0) + (_g == 0) * 1.0
        g_xattn = _g[0]
        g_ffn = _g[1]
        return (x, ctx_768, g_xattn, g_ffn)
    x, ctx_768, g_xattn, g_ffn = _rec_inputs()

    def _L0_xattn_setup():
        import jax, jax.numpy as jnp
        import numpy as np
        IMG_DIM, TXT_DIM, HID = (128, 96, 128)
        B, LQ, LK = (8, 256, 256)
        key = jax.random.key(seed)
        ks = jax.random.split(key, 8)
        s_img = 1.0 / np.sqrt(IMG_DIM)
        s_txt = 1.0 / np.sqrt(TXT_DIM)
        return {'image_features': jax.random.normal(ks[0], (B, LQ, IMG_DIM), jnp.float32), 'text_features': jax.random.normal(ks[1], (B, LK, TXT_DIM), jnp.float32), 'Wq': jax.random.uniform(ks[2], (IMG_DIM, HID), jnp.float32, -s_img, s_img), 'bq': jax.random.uniform(ks[3], (HID,), jnp.float32, -s_img, s_img), 'Wk': jax.random.uniform(ks[4], (TXT_DIM, HID), jnp.float32, -s_txt, s_txt), 'bk': jax.random.uniform(ks[5], (HID,), jnp.float32, -s_txt, s_txt), 'Wv': jax.random.uniform(ks[6], (TXT_DIM, HID), jnp.float32, -s_txt, s_txt), 'bv': jax.random.uniform(ks[7], (HID,), jnp.float32, -s_txt, s_txt)}
    _L0_xattn_all = _L0_xattn_setup()
    _L0_xattn_in = {k: v for k, v in _L0_xattn_all.items() if k in ('Wq', 'bq', 'Wk', 'bk', 'Wv', 'bv')}
    del _L0_xattn_all

    def _L0_ffn_setup():
        import jax, jax.numpy as jnp
        import numpy as np
        BLOCK = 32
        W_BITS = 4
        ACT_BITS = 16

        def act_qdq(x):
            qmax = 2.0 ** (ACT_BITS - 1) - 1.0
            scale = jnp.maximum(jnp.max(jnp.abs(x)) / qmax, 1e-12)
            return jnp.clip(jnp.round(x / scale), -qmax - 1.0, qmax) * scale

        def fixed_qdq_u16(x):
            scale = 1.0 / 65536.0
            return jnp.clip(jnp.round(x / scale), 0.0, 65535.0) * scale

        def lpbq_dequant(w):
            O, I = w.shape
            qmax = 2.0 ** (W_BITS - 1) - 1.0
            wb = w.reshape(O, I // BLOCK, BLOCK)
            s = jnp.maximum(jnp.max(jnp.abs(wb), axis=-1, keepdims=True) / qmax, 1e-12)
            wq = jnp.clip(jnp.round(wb / s), -qmax - 1.0, qmax) * s
            return wq.reshape(O, I)
        key = jax.random.key(seed)
        k1, k2, k3, k4 = jax.random.split(key, 4)
        B, S, H, I = (2, 512, 128, 384)
        x = jax.random.normal(k1, (B, S, H), jnp.float32)
        w_gate = jax.random.normal(k2, (I, H), jnp.float32) * 0.02
        w_up = jax.random.normal(k3, (I, H), jnp.float32) * 0.02
        w_down = jax.random.normal(k4, (H, I), jnp.float32) * 0.02
        return {'x': x, 'w_gate': w_gate, 'w_up': w_up, 'w_down': w_down}
    _L0_ffn_all = _L0_ffn_setup()
    _L0_ffn_in = {k: v for k, v in _L0_ffn_all.items() if k in ('w_gate', 'w_up', 'w_down')}
    del _L0_ffn_all

    def _L1_xattn_setup():
        import jax, jax.numpy as jnp
        import numpy as np
        N_HEADS = 16
        DIMS = 128
        D_CTX = 96
        HEAD = DIMS // N_HEADS
        key = jax.random.key(seed)
        ks = jax.random.split(key, 10)
        s_q = 1.0 / np.sqrt(DIMS)
        s_c = 1.0 / np.sqrt(D_CTX)
        return {'x': jax.random.normal(ks[0], (2, 256, DIMS), jnp.float32), 'context': jax.random.normal(ks[1], (2, 256, D_CTX), jnp.float32), 'w_q': jax.random.normal(ks[2], (DIMS, DIMS), jnp.float32) * s_q, 'b_q': jax.random.normal(ks[3], (DIMS,), jnp.float32) * 0.01, 'w_k': jax.random.normal(ks[4], (D_CTX, DIMS), jnp.float32) * s_c, 'b_k': jax.random.normal(ks[5], (DIMS,), jnp.float32) * 0.01, 'w_v': jax.random.normal(ks[6], (D_CTX, DIMS), jnp.float32) * s_c, 'b_v': jax.random.normal(ks[7], (DIMS,), jnp.float32) * 0.01, 'w_o': jax.random.normal(ks[8], (DIMS, DIMS), jnp.float32) * s_q, 'b_o': jax.random.normal(ks[9], (DIMS,), jnp.float32) * 0.01}
    _L1_xattn_all = _L1_xattn_setup()
    _L1_xattn_in = {k: v for k, v in _L1_xattn_all.items() if k in ('w_q', 'b_q', 'w_k', 'b_k', 'w_v', 'b_v', 'w_o', 'b_o')}
    del _L1_xattn_all

    def _L1_ffn_setup():
        import jax, jax.numpy as jnp
        import numpy as np
        B, S, D, H, E = (4, 256, 128, 16, 4)
        key = jax.random.key(seed)
        ks = jax.random.split(key, 8)
        w = lambda k, shape: jax.random.normal(k, shape, jnp.float32) * 0.02
        return {'x': jax.random.normal(ks[0], (B, S, D), jnp.float32), 'router_w': w(ks[1], (D, E)), 'router_b': jnp.zeros((E,), jnp.float32), 'wq': w(ks[2], (E, D, D)), 'bq': jnp.zeros((E, D), jnp.float32), 'wk': w(ks[3], (E, D, D)), 'bk': jnp.zeros((E, D), jnp.float32), 'wv': w(ks[4], (E, D, D)), 'bv': jnp.zeros((E, D), jnp.float32), 'wo': w(ks[5], (E, D, D)), 'bo': jnp.zeros((E, D), jnp.float32)}
    _L1_ffn_all = _L1_ffn_setup()
    _L1_ffn_in = {k: v for k, v in _L1_ffn_all.items() if k in ('router_w', 'router_b', 'wq', 'bq', 'wk', 'bk', 'wv', 'bv', 'wo', 'bo')}
    del _L1_ffn_all
    return {'x': x, 'ctx_768': ctx_768, 'g_xattn': g_xattn, 'g_ffn': g_ffn, 'L0_xattn_Wq': _L0_xattn_in['Wq'], 'L0_xattn_bq': _L0_xattn_in['bq'], 'L0_xattn_Wk': _L0_xattn_in['Wk'], 'L0_xattn_bk': _L0_xattn_in['bk'], 'L0_xattn_Wv': _L0_xattn_in['Wv'], 'L0_xattn_bv': _L0_xattn_in['bv'], 'L0_ffn_w_gate': _L0_ffn_in['w_gate'], 'L0_ffn_w_up': _L0_ffn_in['w_up'], 'L0_ffn_w_down': _L0_ffn_in['w_down'], 'L1_xattn_w_q': _L1_xattn_in['w_q'], 'L1_xattn_b_q': _L1_xattn_in['b_q'], 'L1_xattn_w_k': _L1_xattn_in['w_k'], 'L1_xattn_b_k': _L1_xattn_in['b_k'], 'L1_xattn_w_v': _L1_xattn_in['w_v'], 'L1_xattn_b_v': _L1_xattn_in['b_v'], 'L1_xattn_w_o': _L1_xattn_in['w_o'], 'L1_xattn_b_o': _L1_xattn_in['b_o'], 'L1_ffn_router_w': _L1_ffn_in['router_w'], 'L1_ffn_router_b': _L1_ffn_in['router_b'], 'L1_ffn_wq': _L1_ffn_in['wq'], 'L1_ffn_bq': _L1_ffn_in['bq'], 'L1_ffn_wk': _L1_ffn_in['wk'], 'L1_ffn_bk': _L1_ffn_in['bk'], 'L1_ffn_wv': _L1_ffn_in['wv'], 'L1_ffn_bv': _L1_ffn_in['bv'], 'L1_ffn_wo': _L1_ffn_in['wo'], 'L1_ffn_bo': _L1_ffn_in['bo']}

def reference(x, ctx_768, g_xattn, g_ffn, L0_xattn_Wq, L0_xattn_bq, L0_xattn_Wk, L0_xattn_bk, L0_xattn_Wv, L0_xattn_bv, L0_ffn_w_gate, L0_ffn_w_up, L0_ffn_w_down, L1_xattn_w_q, L1_xattn_b_q, L1_xattn_w_k, L1_xattn_b_k, L1_xattn_w_v, L1_xattn_b_v, L1_xattn_w_o, L1_xattn_b_o, L1_ffn_router_w, L1_ffn_router_b, L1_ffn_wq, L1_ffn_bq, L1_ffn_wk, L1_ffn_bk, L1_ffn_wv, L1_ffn_bv, L1_ffn_wo, L1_ffn_bo):
    import jax
    import jax.numpy as jnp

    def _L0_xattn_ref(image_features, text_features, Wq, bq, Wk, bk, Wv, bv):
        import jax, jax.numpy as jnp
        import numpy as np
        IMG_DIM, TXT_DIM, HID = (128, 96, 128)
        B, LQ, LK = (8, 256, 256)
        query = jnp.einsum('bqi,ih->bqh', image_features, Wq) + bq
        key = jnp.einsum('bkt,th->bkh', text_features, Wk) + bk
        value = jnp.einsum('bkt,th->bkh', text_features, Wv) + bv
        scale = 1.0 / jnp.sqrt(jnp.asarray(HID, query.dtype))
        scores = jnp.einsum('bqh,bkh->bqk', query, key) * scale
        weights = jax.nn.softmax(scores, axis=-1)
        attended = jnp.einsum('bqk,bkh->bqh', weights, value)
        return attended

    def _L0_ffn_ref(x, w_gate, w_up, w_down):
        import jax, jax.numpy as jnp
        import numpy as np
        BLOCK = 32
        W_BITS = 4
        ACT_BITS = 16

        def act_qdq(x):
            qmax = 2.0 ** (ACT_BITS - 1) - 1.0
            scale = jnp.maximum(jnp.max(jnp.abs(x)) / qmax, 1e-12)
            return jnp.clip(jnp.round(x / scale), -qmax - 1.0, qmax) * scale

        def fixed_qdq_u16(x):
            scale = 1.0 / 65536.0
            return jnp.clip(jnp.round(x / scale), 0.0, 65535.0) * scale

        def lpbq_dequant(w):
            O, I = w.shape
            qmax = 2.0 ** (W_BITS - 1) - 1.0
            wb = w.reshape(O, I // BLOCK, BLOCK)
            s = jnp.maximum(jnp.max(jnp.abs(wb), axis=-1, keepdims=True) / qmax, 1e-12)
            wq = jnp.clip(jnp.round(wb / s), -qmax - 1.0, qmax) * s
            return wq.reshape(O, I)
        x = act_qdq(x)
        up = act_qdq(x @ lpbq_dequant(w_up).T)
        gate = act_qdq(x @ lpbq_dequant(w_gate).T)
        sig = fixed_qdq_u16(jax.nn.sigmoid(gate))
        gate = act_qdq(gate * sig)
        o = act_qdq(gate * up)
        return o @ lpbq_dequant(w_down).T

    def _L1_xattn_ref(x, context, w_q, b_q, w_k, b_k, w_v, b_v, w_o, b_o):
        import jax, jax.numpy as jnp
        import numpy as np
        N_HEADS = 16
        DIMS = 128
        D_CTX = 96
        HEAD = DIMS // N_HEADS
        B, Lq, D = x.shape
        q = x @ w_q + b_q
        k = context @ w_k + b_k
        v = context @ w_v + b_v
        q = q.reshape(B, Lq, N_HEADS, HEAD)
        k = k.reshape(B, -1, N_HEADS, HEAD)
        v = v.reshape(B, -1, N_HEADS, HEAD)
        scale = 1.0 / np.sqrt(HEAD).astype(np.float32)
        scores = jnp.einsum('bqhd,bkhd->bhqk', q, k) * scale
        weights = jax.nn.softmax(scores, axis=-1)
        out = jnp.einsum('bhqk,bkhd->bqhd', weights, v).reshape(B, Lq, D)
        return out @ w_o + b_o

    def _L1_ffn_ref(x, router_w, router_b, wq, bq, wk, bk, wv, bv, wo, bo):
        import jax, jax.numpy as jnp
        import numpy as np
        B, S, D, H, E = (4, 256, 128, 16, 4)
        b, s, d = x.shape
        e_total = router_w.shape[-1]
        h = H
        hd = d // h
        sm_scale = 0.5
        logits = x @ router_w + router_b
        probs = jax.nn.softmax(logits, axis=-1)
        _, top2 = jax.lax.top_k(probs, 2)
        out = jnp.zeros_like(x)
        bidx = jnp.arange(b)[:, None]
        for e in range(e_total):
            member = (top2 == e).any(-1)
            w_tok = jnp.where(member, probs[..., e], 0.0)
            order = jnp.argsort((~member).astype(jnp.int32), axis=-1, stable=True)
            xg = jnp.take_along_axis(x, order[..., None], axis=1)
            validg = jnp.take_along_axis(member, order, axis=1)
            wg = jnp.take_along_axis(w_tok, order, axis=1)
            q = (xg @ wq[e] + bq[e]).reshape(b, s, h, hd)
            k = (xg @ wk[e] + bk[e]).reshape(b, s, h, hd)
            v = (xg @ wv[e] + bv[e]).reshape(b, s, h, hd)
            att = jnp.einsum('bqhd,bkhd->bhqk', q, k) * sm_scale
            att = jnp.where(validg[:, None, None, :], att, -1000000000.0)
            att = jax.nn.softmax(att, axis=-1)
            y = jnp.einsum('bhqk,bkhd->bqhd', att, v).reshape(b, s, d)
            y = y @ wo[e] + bo[e]
            out = out.at[bidx, order].add(wg[..., None] * y)
        return out
    x = x + jnp.tanh(g_xattn[0]) * _L0_xattn_ref(_layernorm(x, axis=-1), ctx_768, L0_xattn_Wq, L0_xattn_bq, L0_xattn_Wk, L0_xattn_bk, L0_xattn_Wv, L0_xattn_bv)
    x = x + jnp.tanh(g_ffn[0]) * _L0_ffn_ref(_layernorm(x, axis=-1), L0_ffn_w_gate, L0_ffn_w_up, L0_ffn_w_down)
    x = x + jnp.tanh(g_xattn[1]) * _L1_xattn_ref(_layernorm(x, axis=-1), ctx_768, L1_xattn_w_q, L1_xattn_b_q, L1_xattn_w_k, L1_xattn_b_k, L1_xattn_w_v, L1_xattn_b_v, L1_xattn_w_o, L1_xattn_b_o)
    x = x + jnp.tanh(g_ffn[1]) * _L1_ffn_ref(_layernorm(x, axis=-1), L1_ffn_router_w, L1_ffn_router_b, L1_ffn_wq, L1_ffn_bq, L1_ffn_wk, L1_ffn_bk, L1_ffn_wv, L1_ffn_bv, L1_ffn_wo, L1_ffn_bo)
    return x

_drawn_inputs = setup_inputs


def setup_inputs(seed=0):
    import zlib

    import numpy as np

    out = dict(_drawn_inputs(seed))
    spreads = {'g_ffn': (-1.0, 0.6),
     'L1_ffn_router_b': (0.0, 0.518),
     'L1_ffn_bq': (0.0, 0.8),
     'L1_ffn_bk': (0.0, 2.0),
     'L1_ffn_bv': (0.0, 0.8),
     'L1_ffn_bo': (0.0, 0.649)}
    factors = {'L0_xattn_bq': 8.0,
     'L0_xattn_bk': 64.0,
     'L0_ffn_w_gate': 7.729,
     'L0_ffn_w_up': 7.323,
     'L0_ffn_w_down': 7.376,
     'L1_xattn_b_q': 52.061,
     'L1_xattn_b_k': 64.0,
     'L1_xattn_b_v': 20.162,
     'L1_xattn_b_o': 18.047,
     'L1_ffn_router_w': 2.834,
     'L1_ffn_wq': 8.0,
     'L1_ffn_wk': 8.0,
     'L1_ffn_wv': 7.752,
     'L1_ffn_wo': 5.503}
    for name, (base, spread) in spreads.items():
        noise = np.random.default_rng([zlib.crc32(name.encode()), seed]).standard_normal(out[name].shape)
        drawn = base * np.exp(spread * noise) if base else spread * noise
        out[name] = jnp.asarray(drawn.astype(out[name].dtype))
    for name, factor in factors.items():
        out[name] = (out[name] * factor).astype(out[name].dtype)
    return out
```

```python
from contextlib import ExitStack

import concourse.bass as bass
from concourse import mybir

F32 = mybir.dt.float32
BF16 = mybir.dt.bfloat16
I32 = mybir.dt.int32
ALU = mybir.AluOpType
ACT = mybir.ActivationFunctionType
AX = mybir.AxisListType
ABSMAX = bass.bass_isa.ReduceOp.absmax

P = 128
ROUND = 1.5 * 2.0**23
Q16 = 32767.0
LN_EPS = 1e-5
NEG = -1e9


def build(nc, x, ctx_768, g_xattn, g_ffn, a_Wq, a_bq, a_Wk, a_bk, a_Wv, a_bv, w_gate, w_up, w_down,
          c_wq, c_bq, c_wk, c_bk, c_wv, c_bv, c_wo, c_bo, router_w, router_b,
          e_wq, e_bq, e_wk, e_bk, e_wv, e_bv, e_wo, e_bo, out):
    B, S, D = x.shape
    _, K, C = ctx_768.shape
    F = w_gate.shape[0]
    E = router_w.shape[1]
    NT = B * S // P
    TB = S // P
    FC = F // P
    K1 = K - P
    CR = B * K
    CT = (CR + P - 1) // P
    CL = CR - (CT - 1) * P
    NBLK = D // 32
    SCALE_A = float(D) ** -0.5
    H, HD = 16, D // 16
    NG = B * E
    SCALE_C, SCALE_E = float(HD) ** -0.5, 0.5
    RING = 3
    QROWS, KROWS = (0, 0, 1, 1, 0, 2), (0, 1, 0, 1, 2, 0)
    MASK = len(QROWS) * HD
    MAXR = MASK + 1
    VW = HD + 1
    FILLS = 14

    with ExitStack() as ctx:
        def sb(name, shape, dt=F32):
            return ctx.enter_context(nc.sbuf_tensor(name, shape, dt))

        def sem(name):
            return ctx.enter_context(nc.semaphore(name))

        X = sb("X", [P, NT, D])
        ident = sb("ident", [P, P])
        ones = sb("ones", [P, P])
        eps = sb("eps", [P, 1])
        gates = sb("gates", [P, 4])
        graw = sb("graw", [P, 4])
        stats = sb("stats", [P, NT, 6])
        mv = sb("mv", [P, NT, 2])
        rstd = sb("rstd", [P, NT])
        ctxT = sb("ctxT", [P, CR])
        bank = [ctx.enter_context(nc.psum_tensor(f"bank{i}", [P, 512], F32)) for i in range(8)]

        QS = sb("QS", [P, H * RING * S], BF16)
        KS = sb("KS", [P, H * RING * S], BF16)
        Wraw = sb("Wraw", [P, 2, D])
        cWv = sb("cWv", [P, D])
        cWo = sb("cWo", [P, D])
        cBo = sb("cBo", [1, D])
        cBq = sb("cBq", [P, 2])
        ARENA = 24 * 1024
        arena = sb("arena", [P, ARENA])
        top = [0]

        def carve(*shape):
            n = 1
            for d in shape:
                n *= d
            a = top[0]
            top[0] += n
            assert top[0] <= ARENA, top[0]
            v = arena[:, a:a + n]
            if len(shape) == 2:
                v = v.rearrange("p (a b) -> p a b", a=shape[0])
            elif len(shape) == 3:
                v = v.rearrange("p (a b c) -> p a b c", a=shape[0], b=shape[1])
            return v

        W3 = carve(3 * FC, D)
        wmax = carve(3 * FC * NBLK)
        winv = carve(3 * FC * NBLK)
        gateT = carve(F)
        upT = carve(F)
        downT = carve(FC, D)
        top_a = top[0]
        ctx_rows = carve(CT, C)
        aWq = carve(D)
        aWk = carve(D)
        aWv = carve(D)
        aBq = carve(1)
        aKT = carve(CR)
        aV = carve(B, 2, D)
        aXn = [carve(TB, D) for _ in range(2)]
        aXT = [carve(S) for _ in range(2)]
        aQT = [carve(S) for _ in range(2)]
        aP = [carve(TB, K) for _ in range(2)]
        aPT = [carve(2, S) for _ in range(2)]
        aMax = carve(B, TB)
        aSum = carve(B, TB)
        aInv = carve(B, TB)
        top[0] = top_a
        fXn = carve(NT, D)
        fXT = carve(NT * P)
        fG = carve(FC, NT * P)
        fU = carve(FC, NT * P)
        fS = [carve(NT * P), carve(NT * P), fXn.rearrange("p n d -> p (n d)")]
        fmax = carve(32)
        fq = carve(16)

        top[0] = 0

        def carve16(*shape):
            n = 1
            for d in shape:
                n *= d
            v = carve(n // 2).bitcast(BF16)
            if len(shape) == 2:
                return v.rearrange("p (a b) -> p a b", a=shape[0])
            return v.rearrange("p (a b c) -> p a b c", a=shape[0], b=shape[1])

        Vr = carve(4 * TB * H * VW)
        V4 = [carve(TB, 4, VW) for _ in range(2)]
        PB = [carve(4 * S) for _ in range(2)]
        Osb = carve(4, S)
        ON = carve(TB, D)
        Usb = carve(S)
        xT = carve(S)
        qf = carve(S)
        kf = carve(CR)
        qp = carve16(3, S)
        kp = carve16(3, CR)
        mallk = carve(TB * TB * H)
        mall = carve(TB, H)
        mres = carve(TB, H)
        nm = carve16(TB, 3, H)
        nmS = carve16(2, S)
        rinv = carve(TB, H)
        identb = carve16(1, P)
        zrow = carve16(2, S)
        mrow = carve16(2, S)
        top_c = top[0]
        iota = carve(S)
        iota16 = carve(S // 2).bitcast(mybir.dt.float16)
        xr = carve16(3 * NT, D)
        G = carve16(TB, S)
        GT = carve(TB, S)
        Wqk = carve(2, D)
        Wv = carve(E, D)
        lXn = Wv
        Wo = carve(E, D)
        bvb = carve(E, D)
        bqk = carve(2, E)
        tokw = carve(4 * 2 * TB)
        isb = carve(TB, 8)
        rw = carve(E)
        rbb = carve(E)
        memb = carve16(TB, NG)
        posm = carve(TB, NG)
        info = carve16(NT * E, 8)
        ebo = carve(D)
        cnt = carve(NG)
        lg, pr, rank, cmp, wgt = (Osb[:, 0, i * NT * E:(i + 1) * NT * E].rearrange("p (n e) -> p n e", n=NT) for i in range(5))
        rsum = Osb[:, 1, 0:NT]
        cntr = Osb[:, 1, P:P + 2 * NG].rearrange("p (a g) -> p a g", a=2)
        onesb = Osb[:, 2, 0:P].bitcast(BF16).rearrange("p (a b) -> p a b", a=2)
        trib = Osb[:, 3, 0:P].bitcast(BF16).rearrange("p (a b) -> p a b", a=2)
        rXn = GT.rearrange("p t s -> p (t s)").rearrange("p (n d) -> p n d", d=D)
        rXT = PB[0]
        wTs = [PB[1][:, b * S:(b + 1) * S] for b in range(B)]
        cnti = sb("cnti", [1, 2 * NG], I32)

        x_loaded = [sem(f"x_loaded{b}") for b in range(B)]
        ctx_loaded = sem("ctx_loaded")
        aw_loaded = sem("aw_loaded")
        g_loaded = sem("g_loaded")
        w3_loaded = sem("w3_loaded")
        consts_ready = sem("consts_ready")
        gates_ready = sem("gates_ready")
        out_stored = sem("out_stored")
        ln_var = sem("ln_var")
        ln_std = sem("ln_std")
        actx_turned = sem("actx_turned")
        actx_ready = sem("actx_ready")
        akv_done = sem("akv_done")
        ak_ready = sem("ak_ready")
        av_ready = sem("av_ready")
        axn_ready = sem("axn_ready")
        axt_done = sem("axt_done")
        axt_ready = sem("axt_ready")
        aq_done = sem("aq_done")
        aq_ready = sem("aq_ready")
        as_done = sem("as_done")
        amax_ready = sem("amax_ready")
        ap_ready = sem("ap_ready")
        apt_done = sem("apt_done")
        apt_ready = sem("apt_ready")
        ao_done = sem("ao_done")
        ax_updated = sem("ax_updated")
        w3_quant = sem("w3_quant")
        w3_turned = sem("w3_turned")
        w3_ready = sem("w3_ready")
        fmax_part = sem("fmax_part")
        fmax_all = sem("fmax_all")
        fxq_ready = sem("fxq_ready")
        fxt_done = sem("fxt_done")
        fxt_ready = sem("fxt_ready")
        fmm_done = sem("fmm_done")
        fmm_kept = sem("fmm_kept")
        fmm_max = sem("fmm_max")
        fgq_ready = sem("fgq_ready")
        fsig_ready = sem("fsig_ready")
        fo_ready = sem("fo_ready")
        fd_done = sem("fd_done")
        fx_updated = sem("fx_updated")

        c_loaded = sem("c_loaded")
        qk_zeroed = sem("qk_zeroed")
        ring_ready = sem("ring_ready")
        c_kv_done = sem("c_kv_done")
        c_k_kept = sem("c_k_kept")
        c_v_kept = sem("c_v_kept")
        c_k_split = sem("c_k_split")
        c_mask = sem("c_mask")
        d_loaded = sem("d_loaded")
        d_consts = sem("d_consts")
        xn_ready = sem("xn_ready")
        xt_full = sem("xt_full")
        xt_kept = sem("xt_kept")
        q_full = sem("q_full")
        q_kept = sem("q_kept")
        k_full = sem("k_full")
        k_kept = sem("k_kept")
        v_full = sem("v_full")
        v_kept = sem("v_kept")
        info_full = sem("info_full")
        info_kept = sem("info_kept")
        tok_ready = sem("tok_ready")
        split_ready = sem("split_ready")
        fill_loaded = sem("fill_loaded")
        w_loaded = sem("w_loaded")
        g_built = sem("g_built")
        gt_built = sem("gt_built")
        m_full = sem("m_full")
        m_free = sem("m_free")
        mall_ready = sem("mall_ready")
        nm_split = sem("nm_split")
        nmt_full = sem("nmt_full")
        nms_full = sem("nms_full")
        nm_loaded = sem("nm_loaded")
        s_full = sem("s_full")
        s_free = sem("s_free")
        av_done = sem("av_done")
        o_free = sem("o_free")
        v4_full = sem("v4_full")
        t_full = sem("t_full")
        t_free = sem("t_free")
        u_full = sem("u_full")
        u_kept = sem("u_kept")
        y_full = sem("y_full")
        x_added = sem("x_added")
        rn_ready = sem("rn_ready")
        mask_ready = sem("mask_ready")
        w_placed = sem("w_placed")
        rx_turned = sem("rx_turned")
        rx_kept = sem("rx_kept")
        r_logits = sem("r_logits")
        r_shift = sem("r_shift")
        r_exp = sem("r_exp")
        r_memb = sem("r_memb")
        r_pos = sem("r_pos")
        r_posm = sem("r_posm")
        r_cnt = sem("r_cnt")
        r_counts = sem("r_counts")
        r_info = sem("r_info")
        r_wt = sem("r_wt")
        r_wt_kept = sem("r_wt_kept")
        r_bias_full = sem("r_bias_full")
        r_bias_added = sem("r_bias_added")
        vr_zeroed = sem("vr_zeroed")
        xr_ready = sem("xr_ready")

        x_v = x.rearrange("b (n p) d -> p (b n) d", p=P)
        out_v = out.rearrange("b (n p) d -> p (b n) d", p=P)
        ctx_v = ctx_768.rearrange("b k c -> (b k) c")

        def column(v):
            return v.rearrange("(d o) -> d o", o=1)

        def row(v):
            return v.rearrange("(o d) -> o d", o=1)

        def by_feature(v):
            return v.rearrange("(h d o) -> d h o", d=HD, o=1)

        QS3 = QS[:, :].rearrange("p (h s) -> p h s", h=H)
        KS3 = KS[:, :].rearrange("p (h s) -> p h s", h=H)
        HS = RING * S
        X2 = X[:, :, :].rearrange("p n d -> p (n d)")

        def shape_of(tq):
            hp = {1: 4, 2: 2, 3: 1, 4: 1}[tq]
            blocks = 4 if tq == 1 else 2
            return hp, 4 // hp, P * tq, blocks, 4 // blocks

        def counter(eng, name, start=0):
            r = eng.alloc_register(name)
            eng.reg_mov(r, start)
            return r

        def wait_count(eng, s, reg, plus=0):
            eng.wait_ge(s, eng.snap(reg) + plus if plus else reg)

        block = ctx.enter_context(nc.Block())

        @block.sync
        def _(sp):
            for b in range(B):
                sp.dma_start(X[:, b * TB:(b + 1) * TB, :], x_v[:, b * TB:(b + 1) * TB, :]).then_inc(x_loaded[b], 16)
            sp.dma_start(W3[:, 0:FC, :], w_gate.rearrange("(c p) i -> p c i", p=P)).then_inc(w3_loaded, 16)
            sp.dma_start(W3[:, FC:2 * FC, :], w_up.rearrange("(c p) i -> p c i", p=P)).then_inc(w3_loaded, 16)
            sp.dma_start(W3[:, 2 * FC:3 * FC, :], w_down.rearrange("p (c i) -> p c i", c=FC)).then_inc(w3_loaded, 16)
            for dst, src in ((Wraw[:, 0, :], c_wq), (Wraw[0:C, 1, :], c_wk), (Wraw[C:C + 1, 1, :], row(c_bk)), (cWv[0:C, :], c_wv),
                             (cWv[C:C + 1, :], row(c_bv)), (cWo[:, :], c_wo), (cBo[:, :], row(c_bo)),
                             ):
                sp.dma_start(dst, src).then_inc(c_loaded, 16)
            sp.dma_start(cBq[:, 0:1], by_feature(c_bq), allow_slow_non_contiguous=True).then_inc(c_loaded, 16)
            sp.wait_ge(ring_ready, 4)
            sp.wait_ge(fx_updated, B)
            one = zrow[0:1, 1:2, :]
            for i in range(RING):
                sp.dma_start(QS3[MASK:MAXR, :, i * S:(i + 1) * S], one.broadcast_to([1, H, S])).then_inc(qk_zeroed, 16)
                for r in range(3):
                    sp.dma_start(KS3[MAXR + r:MAXR + r + 1, :, i * S:(i + 1) * S], one.broadcast_to([1, H, S]))\
                        .then_inc(qk_zeroed, 16)
            sp.wait_ge(qk_zeroed, 16 * 4 * RING)

            def fill(slot, keys, mask):
                for i, (a, b) in enumerate(zip(QROWS, KROWS)):
                    sp.dma_start(QS3[i * HD:(i + 1) * HD, :, bass.ds(slot, S)], qp[:, a, :]).then_inc(fill_loaded, 16)
                    w, src = keys(b)
                    sp.dma_start(KS3[i * HD:(i + 1) * HD, :, bass.ds(slot, w)], src).then_inc(fill_loaded, 16)
                sp.dma_start(QS3[MAXR:MAXR + 3, :, bass.ds(slot, S)], zrow[0:3, 0:1, :].broadcast_to([3, H, S]))\
                    .then_inc(fill_loaded, 16)
                sp.dma_start(KS3[MASK:MAXR, :, bass.ds(slot, S)], mask).then_inc(fill_loaded, 16)

            def maxima(slot):
                sp.dma_start(QS3[MAXR:MAXR + 3, :, bass.ds(slot, S)],
                             nmS[0:3 * H, 0, :]).then_inc(nm_loaded, 16)

            n_split = counter(sp, "n_split")
            n_nms = counter(sp, "n_nms")

            def context_fill(b):
                sp.reg_add(n_split, n_split, 1)
                wait_count(sp, split_ready, n_split)
                sp.wait_ge(c_k_split, 1)
                sp.wait_ge(c_mask, 1)
                fill(sp.snap((b * S) % HS), lambda n: (K, kp[:, n, bass.ds(b * K, K)]),
                     mrow[0:1, 0:1, :].broadcast_to([1, H, S]))

            def send_maxima(g):
                sp.reg_add(n_nms, n_nms, 1)
                wait_count(sp, nms_full, n_nms)
                maxima(sp.snap((g * S) % HS))

            for b in range(3):
                context_fill(b)
            send_maxima(0)
            with sp.Fori(0, B, 1) as b:
                with sp.If(b < B - 1):
                    send_maxima(b + 1)
                with sp.If(b < B - 3):
                    context_fill((b + 3) % B)
                sp.nop()

            for dst, src in ((Wv, e_wv.rearrange("e d h -> d e h")), (Wo, e_wo.rearrange("e d h -> d e h")),
                             (rw, router_w), (rbb, row(router_b).partition_broadcast(P)),
                             (bvb.rearrange("p e d -> p (e d)"), e_bv.rearrange("(o e) d -> o (e d)", o=1).partition_broadcast(P)),
                             (ebo[0:E, :], e_bo)):
                sp.dma_start(dst, src).then_inc(d_loaded, 16)
            for e in range(E):
                sp.dma_start(bqk[:, 0, e:e + 1], by_feature(e_bq[e, :]), allow_slow_non_contiguous=True).then_inc(d_loaded, 16)
                sp.dma_start(bqk[:, 1, e:e + 1], by_feature(e_bk[e, :]), allow_slow_non_contiguous=True).then_inc(d_loaded, 16)
            n_k = counter(sp, "n_k")

            def load_qk(g):
                e = sp.snap(g % E)
                sp.dma_start(Wraw[:, 0, :], e_wq[bass.ds(e, 1), :, :].rearrange("e d h -> (e d) h")).then_inc(w_loaded, 16)
                sp.dma_start(Wraw[:, 1, :], e_wk[bass.ds(e, 1), :, :].rearrange("e d h -> (e d) h")).then_inc(w_loaded, 16)

            def expert_fill(g):
                sp.reg_add(n_split, n_split, 1)
                wait_count(sp, split_ready, n_split)
                wait_count(sp, mask_ready, n_k)
                fill(sp.snap((g * S) % HS), lambda n: (S, kp[:, n, 0:S]),
                     mrow[0:1, 1:2, :].broadcast_to([1, H, S]))

            load_qk(0)
            for g in range(3):
                sp.reg_add(n_k, n_k, 1)
                wait_count(sp, w_placed, n_k, 1)
                load_qk(g + 1)
                expert_fill(g)
            send_maxima(0)
            with sp.Fori(0, NG, 1) as g:
                with sp.If(g < NG - 1):
                    send_maxima(g + 1)
                with sp.If(g < NG - 3):
                    sp.reg_add(n_k, n_k, 1)
                    wait_count(sp, w_placed, n_k, 1)
                    load_qk(g + 4)
                    expert_fill((g + 3) % NG)
                sp.nop()
            sp.wait_ge(x_added, 1 + B + NG)
            sp.wait_ge(w_loaded, 32 * (NG + 1))
            sp.dma_start(out_v, X[:, :, :]).then_inc(out_stored, 16)
            sp.wait_ge(out_stored, 16)

        @block.gpsimd
        def _(pool):
            nc.gpsimd.memset(ones[:, :], 1.0).then_inc(consts_ready, 1)
            nc.gpsimd.memset(eps[:, :], LN_EPS).then_inc(consts_ready, 1)
            pool.drain()
            nc.gpsimd.memset(ctxT[96:97, :], 1.0).then_inc(consts_ready, 1)
            pool.drain()
            nc.gpsimd.memset(ident[:, :], 0.0)
            pool.drain()
            nc.gpsimd.affine_select(out=ident[:, :], in_=ident[:, :], compare_op=ALU.not_equal, fill=1.0,
                                    base=0, pattern=[[-1, P]], channel_multiplier=1).then_inc(consts_ready, 1)
            pool.drain()
            nc.gpsimd.memset(QS[:, :].bitcast(F32), 0.0).then_inc(ring_ready, 1)
            pool.drain()
            nc.gpsimd.memset(KS[:, :].bitcast(F32), 0.0).then_inc(ring_ready, 1)
            for i in range(5):
                pool.wait_ge(fmax_part, i + 1)
                nc.gpsimd.partition_all_reduce(fmax[:, 16 + i:17 + i], fmax[:, i:i + 1], P, ABSMAX)\
                    .then_inc(fmax_all, 1)
            pool.wait_ge(fx_updated, B)
            nc.gpsimd.memset(zrow[:, 0, :], 0.0).then_inc(ring_ready, 1)
            pool.drain()
            nc.gpsimd.memset(zrow[:, 1, :], 1.0).then_inc(ring_ready, 1)
            pool.drain()
            nc.gpsimd.memset(mrow[0:1, 0, 0:K], 0.0)
            pool.drain()
            nc.gpsimd.memset(mrow[0:1, 0, K:S], NEG).then_inc(c_mask, 1)
            pool.drain()
            nc.gpsimd.memset(Vr, 0.0)
            pool.drain()
            nc.gpsimd.memset(Vr.rearrange("p (n w) -> p n w", w=VW)[:, :, HD:VW], 1.0).then_inc(vr_zeroed, 1)
            pool.drain()
            nc.gpsimd.tensor_copy(identb[:, 0, :], ident[:, :])
            pool.drain()

            def split(v, p):
                nc.gpsimd.tensor_tensor(v, v, p[:, 0, :], ALU.subtract)
                pool.drain()
                nc.gpsimd.tensor_copy(p[:, 1, :], v)
                pool.drain()
                return nc.gpsimd.tensor_tensor(p[:, 2, :], v, p[:, 1, :], ALU.subtract)

            def place_weights(rows):
                for i, n in enumerate(rows):
                    t = nc.gpsimd.tensor_copy(Wqk[0:n, i, :].rearrange("p (d h) -> p d h", d=HD),
                                              Wraw[0:n, i, :].rearrange("p (h d) -> p d h", d=HD))
                t.then_inc(w_placed, 1)
                pool.drain()

            pool.wait_ge(c_loaded, 16 * 8)
            place_weights((D, C + 1))
            pool.wait_ge(c_k_kept, 4)
            split(kf, kp).then_inc(c_k_split, 1)

            n_q = counter(pool, "n_q")
            n_mall = counter(pool, "n_mall")

            def split_queries():
                pool.reg_add(n_q, n_q, 1)
                wait_count(pool, q_kept, n_q)
                return split(qf, qp)

            def split_maxima():
                wait_count(pool, mall_ready, n_mall, 1)
                pool.reg_add(n_mall, n_mall, 1)
                nc.gpsimd.tensor_copy(nm[:, :, 0, :], mall)
                pool.drain()
                nc.gpsimd.tensor_tensor(mres, mall, nm[:, :, 0, :], ALU.subtract)
                pool.drain()
                nc.gpsimd.tensor_copy(nm[:, :, 1, :], mres)
                pool.drain()
                nc.gpsimd.tensor_tensor(nm[:, :, 2, :], mres, nm[:, :, 1, :], ALU.subtract).then_inc(nm_split, 1)
                pool.drain()

            for b in range(3):
                split_queries().then_inc(split_ready, 1)
            split_maxima()
            with pool.Fori(0, B, 1) as b:
                with pool.If(b < B - 1):
                    split_maxima()
                with pool.If(b < B - 3):
                    split_queries().then_inc(split_ready, 1)
                pool.nop()

            pool.wait_ge(x_added, 1 + B)
            pool.drain()
            nc.gpsimd.iota(iota, pattern=[[1, S]], base=0, channel_multiplier=0, allow_small_or_imprecise_dtypes=True)\
                .then_inc(d_consts, 1)
            pool.drain()
            nc.gpsimd.tensor_copy(iota16, iota)
            pool.drain()
            nc.gpsimd.memset(onesb[:, 0, :], 1.0).then_inc(d_consts, 1)
            pool.drain()
            nc.gpsimd.affine_select(out=trib[:, 0, :], in_=onesb[:, 0, :], compare_op=ALU.is_gt, fill=0.0, base=0,
                                    pattern=[[1, P]], channel_multiplier=-1).then_inc(d_consts, 1)
            pool.drain()
            nc.gpsimd.iota(rank, pattern=[[0, NT], [1, E]], base=0, channel_multiplier=0,
                           allow_small_or_imprecise_dtypes=True).then_inc(d_consts, 1)
            pool.drain()
            nc.gpsimd.memset(info, 0.0)
            pool.drain()
            nc.gpsimd.iota(info[:, :, 0], pattern=[[0, NT * E]], base=0, channel_multiplier=1,
                           allow_small_or_imprecise_dtypes=True)
            pool.drain()
            nc.gpsimd.iota(info.rearrange("p (b t e) c -> p b t e c", b=B, t=TB)[:, :, :, :, 1], pattern=[[0, B], [1, TB], [0, E]],
                           base=0, channel_multiplier=0, allow_small_or_imprecise_dtypes=True).then_inc(d_consts, 1)
            pool.drain()
            def split_group():
                split_queries()
                wait_count(pool, k_kept, n_w)
                split(kf[:, 0:S], kp[:, :, 0:S]).then_inc(split_ready, 1)
                pool.drain()

            n_w = counter(pool, "n_w")

            def place_expert(first=False):
                if not first:
                    wait_count(pool, k_full, n_w)
                pool.wait_ge(w_loaded, pool.snap(n_w) * 32 + 32)
                pool.reg_add(n_w, n_w, 1)
                place_weights((D, D))

            place_expert(True)
            for g in range(3):
                split_group()
                place_expert()
            split_maxima()
            with pool.Fori(0, NG, 1) as g:
                with pool.If(g < NG - 1):
                    split_maxima()
                with pool.If(g < NG - 3):
                    split_group()
                    place_expert()
                pool.nop()

        @block.tensor
        def _(pe):
            pe.wait_ge(consts_ready, 4)

            pe.wait_ge(ctx_loaded, 32)
            for i in range(CT):
                n = P if i < CT - 1 else CL
                t = nc.tensor.transpose(bank[i // 4][0:C, (i % 4) * P:(i % 4) * P + n], ctx_rows[0:n, i, :], ident[0:n, 0:n])
            t.then_inc(actx_turned, 1)
            pe.wait_ge(aw_loaded, 16 * 6)
            pe.wait_ge(actx_ready, 2)
            for i in range(2):
                nc.tensor.matmul(bank[2 + i][:, 0:CR // 2], aWk[0:C + 1, :], ctxT[0:C + 1, i * CR // 2:(i + 1) * CR // 2],
                                 start=True, stop=True)
            for b in range(B):
                nc.tensor.matmul(bank[4][:, b * D:(b + 1) * D], ctxT[0:C + 1, b * K:b * K + P], aWv[0:C + 1, :],
                                 start=True, stop=True)
                t = nc.tensor.matmul(bank[5][0:K1, b * D:(b + 1) * D], ctxT[0:C + 1, b * K + P:(b + 1) * K], aWv[0:C + 1, :],
                                     start=True, stop=True)
            t.then_inc(akv_done, 1)

            def project(b):
                p = b % 2
                pe.wait_ge(axn_ready, b + 1)
                if b >= 2:
                    pe.wait_ge(ax_updated, b - 1)
                for i in range(TB):
                    t = nc.tensor.transpose(bank[p][:, i * P:(i + 1) * P], aXn[p][:, i, :], ident[:, :])
                t.then_inc(axt_done, 1)
                pe.wait_ge(axt_ready, b + 1)
                if b < 2:
                    pe.wait_ge(ak_ready, 2)
                else:
                    pe.wait_ge(aq_ready, b - 1)
                nc.tensor.matmul(bank[2 + p][:, :], aWq, aXT[p], start=True, stop=True).then_inc(aq_done, 1)

            project(0)
            for b in range(B):
                p = b % 2
                pe.wait_ge(aq_ready, b + 1)
                pe.wait_ge(av_ready, 2)
                if b >= 1:
                    pe.wait_ge(ap_ready, b)
                for i in range(TB):
                    t = nc.tensor.matmul(bank[4 + i // 2][:, (i % 2) * 256:(i % 2) * 256 + K], aQT[p][:, i * P:(i + 1) * P],
                                         aKT[:, b * K:(b + 1) * K], start=True, stop=True)
                t.then_inc(as_done, 1)
                if b + 1 < B:
                    project(b + 1)
                pe.wait_ge(ap_ready, b + 1)
                if b >= 1:
                    pe.wait_ge(apt_ready, 2 * b)
                for i in range(TB):
                    nc.tensor.transpose(bank[6][:, i * P:(i + 1) * P], aP[p][:, i, 0:P], ident[:, :])
                    t = nc.tensor.transpose(bank[7][0:K1, i * P:(i + 1) * P], aP[p][:, i, P:K], ident[:, :])
                t.then_inc(apt_done, 1)
                pe.wait_ge(apt_ready, 2 * b + 2)
                for i in range(TB):
                    nc.tensor.matmul(bank[p][:, i * D:(i + 1) * D], aPT[p][:, 0, i * P:(i + 1) * P], aV[:, b, 0, :],
                                     start=True, stop=False)
                    t = nc.tensor.matmul(bank[p][:, i * D:(i + 1) * D], aPT[p][0:K1, 1, i * P:(i + 1) * P],
                                         aV[0:K1, b, 1, :], start=False, stop=True)
                t.then_inc(ao_done, 1)

            pe.wait_ge(w3_quant, 1)
            for m in range(3):
                if m == 2:
                    pe.wait_ge(ax_updated, B)
                    pe.wait_ge(apt_ready, 2 * B)
                for c in range(FC):
                    t = nc.tensor.transpose(bank[(2, 3, 6)[m]][:, c * P:(c + 1) * P], W3[:, m * FC + c, :], ident[:, :])
                t.then_inc(w3_turned, 1)
            for b in range(B):
                pe.wait_ge(fxq_ready, b + 1)
                for i in range(TB):
                    t = nc.tensor.transpose(bank[(0, 1, 4, 5)[b]][:, i * P:(i + 1) * P], fXn[:, b * TB + i, :], ident[:, :])
                t.then_inc(fxt_done, 1)
            pe.wait_ge(w3_ready, 3)
            n = 0
            for w in (gateT, upT):
                for c in range(FC):
                    for b in range(B):
                        if n < B:
                            pe.wait_ge(fxt_ready, n + 1)
                        if n == 0:
                            pe.wait_ge(fxt_ready, B)
                        if n >= 8:
                            pe.wait_ge(fmm_kept, n - 7)
                            pe.wait_ge(fmm_max, n - 7)
                        nc.tensor.matmul(bank[n % 8][:, :], w[:, c * P:(c + 1) * P], fXT[:, b * S:(b + 1) * S],
                                         start=True, stop=True).then_inc(fmm_done, 1)
                        n += 1
            pe.wait_ge(fo_ready, FC)
            pe.wait_ge(fmm_kept, n)
            pe.wait_ge(fmm_max, n)
            for b in range(B):
                for i in range(TB):
                    for c in range(FC):
                        t = nc.tensor.matmul(bank[b][:, i * D:(i + 1) * D], fG[:, c, (b * TB + i) * P:(b * TB + i + 1) * P],
                                             downT[:, c, :], start=(c == 0), stop=(c == FC - 1))
                t.then_inc(fd_done, 1)

            pe.sem_inc(t_full, 1)
            pe.sem_inc(u_full, 1)
            n_s = counter(pe, "n_s")
            n_m = counter(pe, "n_m")
            n_c = counter(pe, "n_c")
            n_t = counter(pe, "n_t")
            n_g = counter(pe, "n_g")
            n_b = counter(pe, "n_b")
            n_nm = counter(pe, "n_nm")
            n_x = counter(pe, "n_x")
            left = counter(pe, "left")
            lim = counter(pe, "lim")
            kt_m = counter(pe, "kt_m")
            q_at = counter(pe, "q_at")
            k_at = counter(pe, "k_at")
            k_base = counter(pe, "k_base")

            def max_start(g, units, ktiles):
                pe.reg_add(left, left, units)
                pe.reg_mov(lim, ktiles)
                pe.reg_mov(kt_m, 0)
                pe.reg_mov(q_at, pe.snap((g * S) % HS))
                pe.reg_mov(k_at, q_at)
                pe.reg_mov(k_base, q_at)

            def max_bank(c):
                pe.reg_add(n_m, n_m, 1)
                wait_count(pe, m_free, n_m)
                q = pe.snap(q_at, min_val=0, max_val=HS - P)
                k = pe.snap(k_at, min_val=0, max_val=HS - P)
                for j in range(4):
                    t = nc.tensor.matmul(bank[2 + c % 2][:, j * P:(j + 1) * P], QS3[:, 4 * c + j, bass.ds(q, P)],
                                         KS3[:, 4 * c + j, bass.ds(k, P)], start=True, stop=True)
                t.then_inc(m_full, 1)

            def max_next():
                pe.reg_add(k_at, k_at, P)
                pe.reg_add(kt_m, kt_m, 1)
                with pe.If_eq(kt_m, lim):
                    pe.reg_mov(kt_m, 0)
                    pe.reg_mov(k_at, k_base)
                    pe.reg_add(q_at, q_at, P)
                pe.reg_sub(left, left, 1)

            def max_site(c):
                with pe.If(pe.snap(left) > 0):
                    max_bank(c)
                    if c == 3:
                        max_next()

            def max_rest():
                with pe.If(pe.snap(left) > 0):
                    with pe.Fori(0, pe.snap(left), 1):
                        for c in range(4):
                            max_bank(c)
                        max_next()
                pe.nop()

            def attend(g, tq, tk):
                hp, banks, N, blocks, loops = shape_of(tq)
                slot = pe.snap((g * S) % HS)

                def one_pass(it):
                    at = pe.snap(slot + it * (blocks * 4 * HS), min_val=0, max_val=15 * HS)

                    def av(m, issued):
                        cp, kt = m // tk, m % tk
                        exps = pe.snap(n_s)
                        if kt == 0:
                            pe.reg_add(n_c, n_c, 1)
                            wait_count(pe, o_free, n_c)
                            wait_count(pe, v4_full, n_c)
                        pe.wait_ge(s_free, exps + (2 - issued))
                        for j in range(4):
                            t = nc.tensor.matmul(bank[4 + cp % 2][32 * j:32 * j + VW, 0:N], V4[cp % 2][:, kt, j, :],
                                                 PB[m % 2][:, j * N:(j + 1) * N], start=(kt == 0), stop=(kt == tk - 1),
                                                 skip_group_check=True)
                        t.then_inc(av_done, 1)

                    x = 0
                    for m in range(blocks * tk):
                        cp, kt = m // tk, m % tk
                        for i in range(banks):
                            pe.reg_add(n_s, n_s, 1)
                            wait_count(pe, s_free, n_s)
                            for jj in range(hp):
                                h = 4 * cp + i * hp + jj
                                t = nc.tensor.matmul(bank[x % 2][:, jj * N:(jj + 1) * N],
                                                     KS[:, bass.ds(at + (h * HS + kt * P), P)],
                                                     QS[:, bass.ds(at + h * HS, N)], start=True, stop=True)
                            t.then_inc(s_full, 1)
                            max_site(x % 4)
                            x += 1
                            if m and i == min(1, banks - 1):
                                av(m - 1, i + 1)
                    av(blocks * tk - 1, 0)

                if loops == 1:
                    one_pass(0)
                else:
                    with pe.Fori(0, loops, 1) as it:
                        one_pass(it)

            def turn_out(tq):
                pe.wait_ge(o_free, pe.snap(n_c) + 2)
                wait_count(pe, u_kept, n_g, 1)
                wait_count(pe, x_added, n_g, 1)
                for q in range(tq):
                    pe.reg_add(n_t, n_t, 1)
                    wait_count(pe, t_free, n_t)
                    for c in range(4):
                        t = nc.tensor.transpose(bank[6 + q % 2][:, c * P:(c + 1) * P], Osb[:, c, q * P:(q + 1) * P], ident[:, :])
                    t.then_inc(t_full, 1)

            def turn_maxima():
                wait_count(pe, nm_split, n_nm, 1)
                pe.reg_add(n_nm, n_nm, 1)
                for q in range(TB):
                    t = nc.tensor.transpose(bank[0][:, :].bitcast(BF16)[0:3 * H, q * P:(q + 1) * P],
                                            nm[:, q, :, :].rearrange("p r h -> p (r h)"), identb[:, 0, :])
                t.then_inc(nmt_full, 1)

            def ready(n):
                pe.wait_ge(fill_loaded, pe.snap(n * (16 * FILLS)))

            pe.wait_ge(c_loaded, 16 * 8)
            pe.wait_ge(w_placed, 1)
            pe.wait_ge(fx_updated, B)
            pe.wait_ge(vr_zeroed, 1)
            for i in range(2):
                nc.tensor.matmul(bank[i][:, 0:CR // 2], Wqk[0:C + 1, 1, :], ctxT[0:C + 1, i * CR // 2:(i + 1) * CR // 2],
                                 start=True, stop=True)
            for b in range(B):
                nc.tensor.matmul(bank[2][:, b * D:(b + 1) * D], ctxT[0:C + 1, b * K:b * K + P], cWv[0:C + 1, :],
                                 start=True, stop=True)
                t = nc.tensor.matmul(bank[3][0:K1, b * D:(b + 1) * D], ctxT[0:C + 1, b * K + P:(b + 1) * K], cWv[0:C + 1, :],
                                     start=True, stop=True)
            t.then_inc(c_kv_done, 1)
            for i in range(2):
                t = nc.tensor.matmul(bank[4 + i][:, :], zrow[:, 0, 0:P], zrow[:, 0, :], start=True, stop=True)
            t.then_inc(av_done, 2)
            pe.wait_ge(c_v_kept, 2)
            pe.wait_ge(c_k_kept, 4)

            def context_prepare():
                pe.reg_add(n_x, n_x, 1)
                wait_count(pe, xn_ready, n_x)
                for i in range(TB):
                    t = nc.tensor.transpose(bank[2][:, i * P:(i + 1) * P], lXn[:, i, :], ident[:, :])
                t.then_inc(xt_full, 1)
                wait_count(pe, xt_kept, n_x)
                nc.tensor.matmul(bank[1][:, :], Wqk[:, 0, :], xT, start=True, stop=True).then_inc(q_full, 1)

            def finish(g, tq, expert):
                if expert:
                    pe.wait_ge(t_free, pe.snap(n_t) + 2)
                    pe.reg_add(n_e, n_e, 1)
                    wait_count(pe, gt_built, n_e)
                    for q in range(tq):
                        t = nc.tensor.matmul(bank[6][:, :], ON[:, q, :], GT[:, q, :], start=(q == 0), stop=(q == tq - 1))
                else:
                    pe.wait_ge(t_free, pe.snap(n_t) + 2)
                    for q in range(tq):
                        t = nc.tensor.transpose(bank[6][:, q * P:(q + 1) * P], ON[:, q, :], ident[:, :])
                t.then_inc(u_full, 1)

            def project_out(g, expert):
                pe.reg_add(n_g, n_g, 1)
                wait_count(pe, u_kept, n_g, 1)
                for i in range(TB):
                    w = Wo[:, bass.ds(pe.snap(g % E), 1), :].rearrange("p e d -> p (e d)") if expert else cWo[:, :]
                    t = nc.tensor.matmul(bank[7][:, i * D:(i + 1) * D], Usb[:, i * P:(i + 1) * P], w, start=True, stop=expert)
                    if not expert:
                        t = nc.tensor.matmul(bank[7][:, i * D:(i + 1) * D], ones[0:1, :], cBo[:, :], start=False, stop=True)
                t.then_inc(y_full, 1)

            for b in range(3):
                context_prepare()
                wait_count(pe, q_kept, n_x)
            pe.wait_ge(qk_zeroed, 16 * 4 * RING)
            ready(1)
            max_start(0, TB * 2, 2)
            max_rest()
            pe.wait_ge(m_free, pe.snap(n_m) + 2)
            turn_maxima()
            with pe.Fori(0, B, 1) as b:
                with pe.If(b < B - 1):
                    max_start(b + 1, TB * 2, 2)
                    ready(b + 2)
                wait_count(pe, q_kept, n_x)
                pe.wait_ge(nm_loaded, pe.snap(n_b) * 16 + 16)
                pe.reg_add(n_b, n_b, 1)
                attend(b, TB, 2)
                max_rest()
                turn_out(TB)
                pe.wait_ge(m_free, pe.snap(n_m) + 2)
                with pe.If(b < B - 1):
                    turn_maxima()
                with pe.If(b < B - 3):
                    context_prepare()
                finish(b, TB, False)
                project_out(b, False)

            pe.wait_ge(x_added, 1 + B)
            pe.wait_ge(rn_ready, 1)
            for b in range(B):
                for i in range(TB):
                    t = nc.tensor.transpose(bank[b][:, i * P:(i + 1) * P], rXn[:, b * TB + i, :], ident[:, :])
                t.then_inc(rx_turned, 1)
            pe.wait_ge(d_loaded, 16 * 14)
            for b in range(B):
                pe.wait_ge(rx_kept, b + 1)
                for i in range(TB):
                    n = b * TB + i
                    t = nc.tensor.matmul(bank[4][:, n * E:(n + 1) * E], rXT[:, n * P:(n + 1) * P], rw, start=True, stop=True)
            t.then_inc(r_logits, 1)
            pe.wait_ge(r_memb, 1)
            pe.wait_ge(d_consts, 5)
            for t in range(TB):
                for u in range(t + 1):
                    h = nc.tensor.matmul(bank[5][:, t * NG:(t + 1) * NG], (trib if u == t else onesb)[:, 0, :], memb[:, u, :],
                                         start=(u == 0), stop=(u == t))
            h.then_inc(r_pos, 1)
            for t in range(TB):
                h = nc.tensor.matmul(bank[6][0:1, 0:NG], onesb[:, 0, 0:1], memb[:, t, :], start=(t == 0), stop=(t == TB - 1))
            h.then_inc(r_cnt, 1)
            for n in range(NT):
                t = nc.tensor.transpose(bank[n // 4][0:E, (n % 4) * P:(n % 4 + 1) * P], wgt[:, n, :], ident[:, :])
                if n % 4 == 3:
                    t.then_inc(r_wt, 1)
            for b in range(B):
                pe.wait_ge(r_wt_kept, b + 1)
                if b == 0:
                    pe.wait_ge(r_counts, 1)
                    pe.wait_ge(r_wt_kept, B)
                for i in range(TB):
                    t = nc.tensor.matmul(bank[b][:, i * D:(i + 1) * D], wTs[b][0:E, i * P:(i + 1) * P], ebo[0:E, :],
                                         start=True, stop=True)
                t.then_inc(r_bias_full, 1)
            pe.wait_ge(r_bias_added, B)
            pe.wait_ge(r_info, 1)
            pe.wait_ge(xr_ready, 1)
            n_d = counter(pe, "n_d")
            n_e = counter(pe, "n_e")

            def expert_prepare(g):
                b4 = pe.snap((g // E) * TB)
                pe.reg_add(n_x, n_x, 1)
                pe.reg_add(n_d, n_d, 1)
                wait_count(pe, g_built, n_d)
                for t in range(TB):
                    for r in range(3):
                        h = nc.tensor.matmul(bank[2][:, :], xr[:, bass.ds(pe.snap(b4 + (r * NT + t)), 1), :].rearrange("p n d -> p (n d)"),
                                             G[:, t, :], start=(t == 0 and r == 0), stop=(t == TB - 1 and r == 2))
                h.then_inc(xt_full, 1)
                for k in range(TB):
                    for t in range(TB):
                        h = nc.tensor.matmul(bank[3][:, k * 8:(k + 1) * 8], G[:, t, k * P:(k + 1) * P],
                                             info[:, bass.ds(pe.snap((b4 + t) * E + g % E), 1), :].rearrange("p n c -> p (n c)"),
                                             start=(t == 0), stop=(t == TB - 1))
                h.then_inc(info_full, 1)
                wait_count(pe, xt_kept, n_x)
                wait_count(pe, w_placed, n_d, 1)
                nc.tensor.matmul(bank[1][:, :], Wqk[:, 0, :], xT, start=True, stop=True).then_inc(q_full, 1)
                nc.tensor.matmul(bank[2][:, :], Wqk[:, 1, :], xT, start=True, stop=True).then_inc(k_full, 1)
                wait_count(pe, info_kept, n_d)
                for k in range(TB):
                    h = nc.tensor.matmul(bank[3][:, k * P:(k + 1) * P], xT[:, k * P:(k + 1) * P],
                                         Wv[:, bass.ds(pe.snap(g % E), 1), :].rearrange("p e d -> p (e d)"), start=True, stop=True)
                h.then_inc(v_full, 1)

            def prepared():
                wait_count(pe, q_kept, n_x)
                wait_count(pe, k_kept, n_d)
                wait_count(pe, v_kept, n_d)

            def tiles(g):
                return pe.value_load(cnti[0:1, bass.ds(g, 1)], min_val=0, max_val=TB)

            tn = tiles(0)
            for g in range(3):
                expert_prepare(g)
                prepared()
            ready(B + 1)
            max_start(0, tn * tn, tn)
            max_rest()
            pe.wait_ge(m_free, pe.snap(n_m) + 2)
            turn_maxima()
            with pe.Fori(0, NG, 1) as g:
                tc = tiles(g)
                tn = tiles(g + 1)
                prepared()
                pe.wait_ge(nm_loaded, pe.snap(n_b) * 16 + 16)
                pe.reg_add(n_b, n_b, 1)
                with pe.If(g < NG - 1):
                    ready(g + (B + 2))
                max_start(g + 1, tn * tn, tn)
                for v in range(1, TB + 1):
                    with pe.If(tc == v):
                        attend(g, v, v)
                        max_rest()
                        turn_out(v)
                pe.wait_ge(m_free, pe.snap(n_m) + 2)
                with pe.If(g < NG - 1):
                    turn_maxima()
                with pe.If(g < NG - 3):
                    expert_prepare((g + 3) % NG)
                for v in range(1, TB + 1):
                    with pe.If(tc == v):
                        finish(g, v, True)
                project_out(g, True)

        @block.scalar
        def _(act):
            act.dma_start(ctx_rows[:, 0:CT - 1, :], ctx_v[0:(CT - 1) * P, :].rearrange("(n p) c -> p n c", p=P))\
                .then_inc(ctx_loaded, 16)
            act.dma_start(ctx_rows[0:CL, CT - 1, :], ctx_v[(CT - 1) * P:CR, :]).then_inc(ctx_loaded, 16)
            act.dma_start(graw[:, 0:2], row(g_xattn).partition_broadcast(P)).then_inc(g_loaded, 16)
            act.dma_start(graw[:, 2:4], row(g_ffn).partition_broadcast(P)).then_inc(g_loaded, 16)
            act.dma_start(aWq, a_Wq).then_inc(aw_loaded, 16)
            act.dma_start(aBq, column(a_bq)).then_inc(aw_loaded, 16)
            act.dma_start(aWk[0:C, :], a_Wk).then_inc(aw_loaded, 16)
            act.dma_start(aWk[C:C + 1, :], row(a_bk)).then_inc(aw_loaded, 16)
            act.dma_start(aWv[0:C, :], a_Wv).then_inc(aw_loaded, 16)
            act.dma_start(aWv[C:C + 1, :], row(a_bv)).then_inc(aw_loaded, 16)
            act.wait_ge(g_loaded, 32)
            nc.scalar.activation(gates[:, :], graw[:, :], ACT.Tanh).then_inc(gates_ready, 1)
            act.wait_ge(actx_turned, 1)
            nc.scalar.copy(ctxT[0:C, 0:512], bank[0][0:C, :]).then_inc(actx_ready, 1)
            nc.scalar.copy(ctxT[0:C, 512:CR], bank[1][0:C, 0:CR - 512]).then_inc(actx_ready, 1)
            act.wait_ge(consts_ready, 4)
            act.wait_ge(ln_var, 1)
            nc.scalar.activation(rstd[:, :], mv[:, :, 1], ACT.Sqrt, bias=eps[:, :]).then_inc(ln_std, 1)
            act.wait_ge(akv_done, 1)
            for i in range(2):
                nc.scalar.copy(aKT[:, i * CR // 2:(i + 1) * CR // 2], bank[2 + i][:, 0:CR // 2]).then_inc(ak_ready, 1)

            def project(b):
                p = b % 2
                act.wait_ge(axt_done, b + 1)
                if b >= 2:
                    act.wait_ge(aq_done, b - 1)
                nc.scalar.copy(aXT[p], bank[p][:, :]).then_inc(axt_ready, 1)
                act.wait_ge(aq_done, b + 1)
                if b >= 2:
                    act.wait_ge(as_done, b - 1)
                nc.scalar.activation(aQT[p], bank[2 + p][:, :], ACT.Identity, bias=aBq).then_inc(aq_ready, 1)

            project(0)
            for b in range(B):
                p = b % 2
                if b + 1 < B:
                    project(b + 1)
                act.wait_ge(amax_ready, b + 1)
                if b >= 2:
                    act.wait_ge(apt_done, b - 1)
                for i in range(TB):
                    t = nc.scalar.activation(aP[p][:, i, :], bank[4 + i // 2][:, (i % 2) * 256:(i % 2) * 256 + K], ACT.Exp,
                                             bias=aMax[:, b, i:i + 1], scale=SCALE_A, accum_out=aSum[:, b, i:i + 1])
                t.then_inc(ap_ready, 1)

            for m, dst in enumerate((gateT, upT, downT.rearrange("p a b -> p (a b)"))):
                act.wait_ge(w3_turned, m + 1)
                nc.scalar.copy(dst, bank[(2, 3, 6)[m]][:, 0:F]).then_inc(w3_ready, 1)
            act.wait_ge(ln_var, 2)
            act.wait_ge(axn_ready, B)
            nc.scalar.activation(rstd[:, :], mv[:, :, 1], ACT.Sqrt, bias=eps[:, :]).then_inc(ln_std, 1)
            for b in range(B):
                act.wait_ge(fxt_done, b + 1)
                nc.scalar.copy(fXT[:, b * S:(b + 1) * S], bank[(0, 1, 4, 5)[b]][:, :]).then_inc(fxt_ready, 1)
            n = 0
            for dst in (fG, fU):
                for c in range(FC):
                    for b in range(B):
                        act.wait_ge(fmm_done, n + 1)
                        act.wait_ge(fmm_max, n + 1)
                        nc.scalar.copy(dst[:, c, b * S:(b + 1) * S], bank[n % 8][:, :]).then_inc(fmm_kept, 1)
                        n += 1
            for c in range(FC):
                act.wait_ge(fgq_ready, c + 1)
                nc.scalar.activation(fS[c], fG[:, c, :], ACT.Sigmoid).then_inc(fsig_ready, 1)

            a_mac = counter(act, "a_mac")
            a_s = counter(act, "a_s")
            a_t = counter(act, "a_t")
            a_x = counter(act, "a_x")
            a_nm = counter(act, "a_nm")
            a_u = counter(act, "a_u")
            act.wait_ge(fx_updated, B)
            act.sem_inc(s_free, 2)
            act.sem_inc(o_free, 2)
            act.sem_inc(u_kept, 1)
            act.wait_ge(ln_var, 3)
            nc.scalar.activation(rstd[:, :], mv[:, :, 1], ACT.Sqrt, bias=eps[:, :]).then_inc(ln_std, 1)
            act.wait_ge(c_loaded, 16 * 8)
            nc.scalar.activation(cBq[:, 1:2], cBq[:, 0:1], ACT.Copy, scale=SCALE_C)
            act.wait_ge(c_kv_done, 1)
            for i in range(2):
                half = slice(i * CR // 2, (i + 1) * CR // 2)
                nc.scalar.copy(kf[:, half], bank[i][:, 0:CR // 2]).then_inc(c_k_kept, 1)
                nc.scalar.copy(kp[:, 0, half], bank[i][:, 0:CR // 2]).then_inc(c_k_kept, 1)
            act.drain()

            def keep_queries(scale, bias):
                wait_count(act, q_full, a_x)
                nc.scalar.activation(qf, bank[1][:, :], ACT.Identity, bias=bias, scale=scale)
                nc.scalar.activation(qp[:, 0, :], bank[1][:, :], ACT.Identity, bias=bias, scale=scale).then_inc(q_kept, 1)

            def keep_x(first=False):
                if not first:
                    act.wait_ge(fill_loaded, act.snap(a_x) * (16 * FILLS))
                act.reg_add(a_x, a_x, 1)
                wait_count(act, xt_full, a_x)
                nc.scalar.copy(xT, bank[2][:, :]).then_inc(xt_kept, 1)

            def context_prepare(first=False):
                keep_x(first)
                keep_queries(SCALE_C, cBq[:, 1:2])

            def keep_maxima(first=False):
                if not first:
                    act.wait_ge(nm_loaded, act.snap(a_nm) * 16)
                act.reg_add(a_nm, a_nm, 1)
                wait_count(act, nmt_full, a_nm)
                nc.scalar.copy(nmS[0:3 * H, 0, :], bank[0][:, :].bitcast(BF16)[0:3 * H, 0:S]).then_inc(nms_full, 1)

            def attend(tq, tk):
                hp, banks, N, blocks, loops = shape_of(tq)

                def keep_output(c0, cp, plus):
                    act.wait_ge(av_done, act.snap(a_mac) + plus)
                    dst = Osb[:, cp:cp + 1, 0:N] if loops == 1 else Osb[:, bass.ds(act.snap(c0 + cp), 1), 0:N]
                    nc.scalar.copy(dst.rearrange("p c n -> p (c n)"), bank[4 + cp % 2][:, 0:N]).then_inc(o_free, 1)

                def one_pass(c0):
                    x = 0
                    for m in range(blocks * tk):
                        act.reg_add(a_mac, a_mac, 1)
                        for i in range(banks):
                            act.reg_add(a_s, a_s, 1)
                            wait_count(act, s_full, a_s)
                            if i == 0:
                                wait_count(act, av_done, a_mac)
                            nc.scalar.activation(PB[m % 2][:, i * hp * N:(i + 1) * hp * N], bank[x % 2][:, 0:hp * N], ACT.Exp)\
                                .then_inc(s_free, 1)
                            x += 1
                            if m and m % tk == 0 and i == min(1, banks - 1):
                                keep_output(c0, m // tk - 1, 1)
                    keep_output(c0, blocks - 1, 2)

                wait_count(act, t_full, a_t, 1)
                if loops == 1:
                    one_pass(0)
                else:
                    with act.Fori(0, loops, 1) as it:
                        one_pass(it * blocks)
                act.reg_add(a_t, a_t, tq)

            def keep_tokens():
                act.reg_add(a_u, a_u, 1)
                wait_count(act, u_full, a_u, 1)
                nc.scalar.copy(Usb, bank[6][:, :]).then_inc(u_kept, 1)

            for b in range(3):
                context_prepare(b == 0)
            keep_maxima(True)
            with act.Fori(0, B, 1) as b:
                attend(TB, 2)
                with act.If(b < B - 1):
                    keep_maxima()
                with act.If(b < B - 3):
                    context_prepare()
                keep_tokens()

            act.wait_ge(ln_var, 4)
            nc.scalar.activation(rstd[:, :], mv[:, :, 1], ACT.Sqrt, bias=eps[:, :]).then_inc(ln_std, 1)
            for b in range(B):
                act.wait_ge(rx_turned, b + 1)
                nc.scalar.copy(rXT[:, b * S:(b + 1) * S], bank[b][:, :]).then_inc(rx_kept, 1)
            act.wait_ge(r_shift, 1)
            nc.scalar.activation(pr, lg, ACT.Exp).then_inc(r_exp, 1)
            for b in range(B):
                act.wait_ge(r_wt, b + 1)
                nc.scalar.copy(wTs[b][0:E, :], bank[b][0:E, :]).then_inc(r_wt_kept, 1)
            act.wait_ge(d_loaded, 16 * 14)
            nc.scalar.activation(bqk[:, 0, :], bqk[:, 0, :], ACT.Copy, scale=SCALE_E)
            act.wait_ge(r_counts, 1)
            a_d = counter(act, "a_d")

            def expert_prepare(g):
                e = act.snap(g % E)
                act.reg_add(a_d, a_d, 1)
                keep_x()
                keep_queries(SCALE_E, bqk[:, 0, bass.ds(e, 1)])
                wait_count(act, k_full, a_d)
                nc.scalar.activation(kf[:, 0:S], bank[2][:, :], ACT.Identity, bias=bqk[:, 1, bass.ds(e, 1)])
                nc.scalar.activation(kp[:, 0, 0:S], bank[2][:, :], ACT.Identity, bias=bqk[:, 1, bass.ds(e, 1)])\
                    .then_inc(k_kept, 1)

            act.drain()
            for g in range(3):
                expert_prepare(g)
            keep_maxima()
            with act.Fori(0, NG, 1) as g:
                tc = act.value_load(cnti[0:1, bass.ds(g, 1)], min_val=0, max_val=TB)
                for v in range(1, TB + 1):
                    with act.If(tc == v):
                        attend(v, v)
                with act.If(g < NG - 1):
                    keep_maxima()
                with act.If(g < NG - 3):
                    expert_prepare((g + 3) % NG)
                keep_tokens()

        @block.vector
        def _(dve):
            def layer_norm_stats():
                for n in range(NT):
                    nc.vector.bn_stats(stats[:, n, :], X[:, n, :])
                dve.drain()
                for n in range(NT):
                    t = nc.vector.bn_aggr(mv[:, n, :], stats[:, n, :])
                t.then_inc(ln_var, 1)

            def normalise(dst, n):
                return nc.vector.tensor_scalar(dst, X[:, n, :], mv[:, n, 0:1], rstd[:, n:n + 1], ALU.subtract, ALU.mult)

            for b in range(B):
                dve.wait_ge(x_loaded[b], 16)
            layer_norm_stats()
            dve.wait_ge(ln_std, 1)
            nc.vector.reciprocal(rstd[:, :], rstd[:, :])
            dve.drain()

            def feed(b):
                p = b % 2
                if b >= 2:
                    dve.wait_ge(axt_done, b - 1)
                for i in range(TB):
                    t = normalise(aXn[p][:, i, :], b * TB + i)
                t.then_inc(axn_ready, 1)

            feed(0)
            dve.wait_ge(akv_done, 1)
            nc.vector.tensor_copy(aV[:, :, 0, :], bank[4][:, :].rearrange("p (b d) -> p b d", b=B)).then_inc(av_ready, 1)
            nc.vector.tensor_copy(aV[0:K1, :, 1, :], bank[5][0:K1, :].rearrange("p (b d) -> p b d", b=B))\
                .then_inc(av_ready, 1)
            feed(1)

            dve.wait_ge(w3_loaded, 48)
            blocks = W3.rearrange("p c (n i) -> p (c n) i", i=32)
            wmax_b = wmax.rearrange("p (n o) -> p n o", o=1).broadcast_to([P, 3 * FC * NBLK, 32])
            winv_b = winv.rearrange("p (n o) -> p n o", o=1).broadcast_to([P, 3 * FC * NBLK, 32])
            nc.vector.tensor_reduce(wmax, blocks, AX.X, ALU.max, apply_absolute_value=True)
            dve.drain()
            nc.vector.tensor_scalar(wmax, wmax, 1.0 / 7.0, 1e-12, ALU.mult, ALU.max)
            dve.drain()
            nc.vector.reciprocal(winv, wmax)
            dve.drain()
            nc.vector.tensor_tensor(blocks, blocks, winv_b, ALU.mult)
            dve.drain()
            nc.vector.tensor_scalar(W3, W3, ROUND, ROUND, ALU.add, ALU.subtract)
            dve.drain()
            nc.vector.tensor_tensor(blocks, blocks, wmax_b, ALU.mult).then_inc(w3_quant, 1)

            for b in range(B):
                p = b % 2
                dve.wait_ge(as_done, b + 1)
                for j in range(2):
                    nc.vector.tensor_reduce(aMax[:, b, 2 * j:2 * j + 2],
                                            bank[4 + j][:, :].rearrange("p (i k) -> p i k", i=2)[:, :, 0:K], AX.X, ALU.max)
                dve.drain()
                nc.vector.tensor_scalar(aMax[:, b, :], aMax[:, b, :], -SCALE_A, None, ALU.mult).then_inc(amax_ready, 1)
                if b + 2 < B:
                    feed(b + 2)
                dve.wait_ge(apt_done, b + 1)
                if b >= 2:
                    dve.wait_ge(ao_done, b - 1)
                nc.vector.tensor_copy(aPT[p][:, 0, :], bank[6][:, :]).then_inc(apt_ready, 1)
                nc.vector.tensor_copy(aPT[p][0:K1, 1, :], bank[7][0:K1, :]).then_inc(apt_ready, 1)
                nc.vector.reciprocal(aInv[:, b, :], aSum[:, b, :])
                dve.wait_ge(gates_ready, 1)
                dve.drain()
                nc.vector.tensor_scalar(aInv[:, b, :], aInv[:, b, :], gates[:, 0:1], None, ALU.mult)
                dve.drain()
                dve.wait_ge(ao_done, b + 1)
                for i in range(TB):
                    t = nc.vector.scalar_tensor_tensor(out=X[:, b * TB + i, :], in0=bank[p][:, i * D:(i + 1) * D],
                                                       scalar=aInv[:, b, i:i + 1], in1=X[:, b * TB + i, :],
                                                       op0=ALU.mult, op1=ALU.add)
                t.then_inc(ax_updated, 1)

            def quantiser(i):
                dve.wait_ge(fmax_all, i + 1)
                nc.vector.tensor_scalar(fq[:, 2 * i:2 * i + 1], fmax[:, 16 + i:17 + i], 1.0 / Q16, 1e-12, ALU.mult, ALU.max)
                dve.drain()
                nc.vector.reciprocal(fq[:, 2 * i + 1:2 * i + 2], fq[:, 2 * i:2 * i + 1])
                dve.drain()

            def quantise(v, i):
                nc.vector.tensor_scalar(v, v, fq[:, 2 * i + 1:2 * i + 2], ROUND, ALU.mult, ALU.add)
                dve.drain()
                return nc.vector.tensor_scalar(v, v, ROUND, fq[:, 2 * i:2 * i + 1], ALU.subtract, ALU.mult)

            dve.drain()
            layer_norm_stats()
            dve.wait_ge(ln_std, 2)
            nc.vector.reciprocal(rstd[:, :], rstd[:, :])
            dve.drain()
            for n in range(NT):
                normalise(fXn[:, n, :], n)
            dve.drain()
            nc.vector.tensor_reduce(fmax[:, 0:1], fXn, AX.XY, ALU.max, apply_absolute_value=True).then_inc(fmax_part, 1)
            quantiser(0)
            for b in range(B):
                quantise(fXn[:, b * TB:(b + 1) * TB, :], 0).then_inc(fxq_ready, 1)
            for n in range(2 * FC * B):
                dve.wait_ge(fmm_done, n + 1)
                nc.vector.tensor_reduce(fmax[:, 8:9] if n % (FC * B) == 0 else fmax[:, 9:10], bank[n % 8][:, :], AX.X,
                                        ALU.max, apply_absolute_value=True).then_inc(fmm_max, 1)
                dve.drain()
                if n % (FC * B):
                    t = nc.vector.tensor_tensor(fmax[:, 8:9], fmax[:, 8:9], fmax[:, 9:10], ALU.max)
                    dve.drain()
                if n % (FC * B) == FC * B - 1:
                    m = 1 + n // (FC * B)
                    nc.vector.tensor_copy(fmax[:, m:m + 1], fmax[:, 8:9]).then_inc(fmax_part, 1)
                    dve.drain()
            quantiser(1)
            dve.wait_ge(fmm_kept, 2 * FC * B)
            for c in range(FC):
                quantise(fG[:, c, :], 1).then_inc(fgq_ready, 1)
            quantiser(2)
            for c in range(FC):
                quantise(fU[:, c, :], 2)
            for c in range(FC):
                dve.wait_ge(fsig_ready, c + 1)
                nc.vector.tensor_scalar(fS[c], fS[c], 65536.0, ROUND, ALU.mult, ALU.add)
                dve.drain()
                nc.vector.tensor_scalar(fS[c], fS[c], ROUND, 65535.0, ALU.subtract, ALU.min)
                dve.drain()
                nc.vector.scalar_tensor_tensor(out=fG[:, c, :], in0=fS[c], scalar=1.0 / 65536.0, in1=fG[:, c, :],
                                               op0=ALU.mult, op1=ALU.mult)
                dve.drain()
                nc.vector.tensor_reduce(fmax[:, 8 + c:9 + c], fG[:, c, :], AX.X, ALU.max, apply_absolute_value=True)
            dve.drain()
            nc.vector.tensor_reduce(fmax[:, 3:4], fmax[:, 8:8 + FC], AX.X, ALU.max).then_inc(fmax_part, 1)
            quantiser(3)
            for c in range(FC):
                quantise(fG[:, c, :], 3)
                dve.drain()
                nc.vector.tensor_tensor(fG[:, c, :], fG[:, c, :], fU[:, c, :], ALU.mult)
                dve.drain()
                nc.vector.tensor_reduce(fmax[:, 8 + c:9 + c], fG[:, c, :], AX.X, ALU.max, apply_absolute_value=True)
            dve.drain()
            nc.vector.tensor_reduce(fmax[:, 4:5], fmax[:, 8:8 + FC], AX.X, ALU.max).then_inc(fmax_part, 1)
            quantiser(4)
            for c in range(FC):
                quantise(fG[:, c, :], 4).then_inc(fo_ready, 1)
            for b in range(B):
                dve.wait_ge(fd_done, b + 1)
                nc.vector.scalar_tensor_tensor(out=X[:, b * TB:(b + 1) * TB, :].rearrange("p n d -> p (n d)"),
                                               in0=bank[b][:, :], scalar=gates[:, 2:3],
                                               in1=X[:, b * TB:(b + 1) * TB, :].rearrange("p n d -> p (n d)"),
                                               op0=ALU.mult, op1=ALU.add).then_inc(fx_updated, 1)

            v_m = counter(dve, "v_m")
            v_mac = counter(dve, "v_mac")
            v_t = counter(dve, "v_t")
            v_x = counter(dve, "v_x")
            v_y = counter(dve, "v_y")
            v_mall = counter(dve, "v_mall")
            left = counter(dve, "v_left")
            lim = counter(dve, "v_lim")
            kt_m = counter(dve, "v_kt")
            q_out = counter(dve, "v_q")
            at_m = counter(dve, "v_at")
            dve.sem_inc(m_free, 2)
            dve.sem_inc(t_free, 2)
            dve.sem_inc(x_added, 1)
            Vs = Vr.rearrange("p (s k w) -> p s k w", s=4, k=TB)
            Vh = Vr.rearrange("p (s k h w) -> p s k h w", s=4, k=TB, h=H)
            maxima = mallk.rearrange("p (k q) -> p q k", k=TB)

            def max_start(units, ktiles):
                dve.reg_mov(left, units)
                dve.reg_mov(lim, ktiles)
                dve.reg_mov(kt_m, 0)
                dve.reg_mov(q_out, 0)
                dve.reg_mov(at_m, 0)
                nc.vector.memset(mallk, -1e30)
                dve.drain()

            def max_bank(c):
                dve.reg_add(v_m, v_m, 1)
                wait_count(dve, m_full, v_m)
                nc.vector.tensor_reduce(mallk[:, bass.ds(dve.snap(at_m, min_val=0, max_val=TB * TB * H - H) + 4 * c, 4)],
                                        bank[2 + c % 2][:, :].rearrange("p (j k) -> p j k", j=4), AX.X, ALU.max)\
                    .then_inc(m_free, 1)

            def max_next():
                dve.reg_add(at_m, at_m, TB * H)
                dve.reg_add(kt_m, kt_m, 1)
                with dve.If_eq(kt_m, lim):
                    dve.reg_mov(kt_m, 0)
                    dve.reg_add(q_out, q_out, H)
                    dve.reg_mov(at_m, q_out)
                dve.reg_sub(left, left, 1)

            def max_site(c):
                with dve.If(dve.snap(left) > 0):
                    max_bank(c)
                    if c == 3:
                        max_next()

            def max_rest():
                with dve.If(dve.snap(left) > 0):
                    with dve.Fori(0, dve.snap(left), 1):
                        for c in range(4):
                            max_bank(c)
                        max_next()
                dve.nop()

            def max_end(first=False):
                if not first:
                    wait_count(dve, nm_split, v_mall)
                dve.reg_add(v_mall, v_mall, 1)
                dve.drain()
                nc.vector.tensor_reduce(mall.rearrange("p q h -> p (q h)"), maxima, AX.X, ALU.max)
                dve.drain()
                nc.vector.tensor_scalar(mall, mall, -1.0, None, ALU.mult).then_inc(mall_ready, 1)

            def attend(slot, tq, tk):
                hp, banks, N, blocks, loops = shape_of(tq)

                def values(c0, c, plus):
                    dve.wait_ge(av_done, dve.snap(v_mac) + plus)
                    at = (c0 + c) * (4 * VW)
                    nc.vector.tensor_copy(V4[c % 2][:, 0:tk, :, :].rearrange("p k j w -> p k (j w)"),
                                          Vs[:, bass.ds(slot, 1), 0:tk, bass.ds(dve.snap(at) if loops > 1 else at, 4 * VW)]
                                          .rearrange("p s k w -> p (s k) w")).then_inc(v4_full, 1)

                def one_pass(c0):
                    values(c0, 0, 2)
                    values(c0, 1, 2)
                    x = 0
                    for m in range(blocks * tk):
                        for i in range(banks):
                            max_site(x % 4)
                            x += 1
                            if m and m % tk == 0 and i == min(1, banks - 1) and m // tk + 1 < blocks:
                                values(c0, m // tk + 1, 2 + m)
                    dve.reg_add(v_mac, v_mac, blocks * tk)

                if loops == 1:
                    one_pass(0)
                else:
                    with dve.Fori(0, loops, 1) as it:
                        one_pass(it * blocks)

            def normalise_out(tq, weight):
                dve.drain()
                for q in range(tq):
                    dve.reg_add(v_t, v_t, 1)
                    wait_count(dve, t_full, v_t, 1)
                    T = bank[6 + q % 2][:, :].rearrange("p (h w) -> p h w", h=H)
                    nc.vector.reciprocal(rinv[:, q, :], T[:, :, HD])
                    dve.drain()
                    if weight is not None:
                        nc.vector.tensor_scalar(rinv[:, q, :], rinv[:, q, :], tokw[:, bass.ds(dve.snap(weight + q), 1)], None, ALU.mult)
                        dve.drain()
                    nc.vector.tensor_tensor(ON[:, q, :].rearrange("p (h d) -> p h d", h=H), T[:, :, 0:HD],
                                            rinv[:, q, :].rearrange("p (h o) -> p h o", o=1).broadcast_to([P, H, HD]), ALU.mult)\
                        .then_inc(t_free, 1)

            def add_out(b, gate):
                dve.reg_add(v_y, v_y, 1)
                wait_count(dve, y_full, v_y)
                xb = X2[:, bass.ds(dve.snap(b * S), S)]
                nc.vector.scalar_tensor_tensor(out=xb, in0=bank[7][:, :], scalar=gate, in1=xb, op0=ALU.mult, op1=ALU.add)\
                    .then_inc(x_added, 1)

            def feed_context(b):
                if not (isinstance(b, int) and b == 0):
                    wait_count(dve, xt_full, v_x)
                dve.reg_add(v_x, v_x, 1)
                for i in range(TB):
                    if isinstance(b, int):
                        t = normalise(lXn[:, i, :], b * TB + i)
                    else:
                        n = dve.snap(b * TB + i)
                        t = nc.vector.tensor_scalar(lXn[:, i, :], X2[:, bass.ds(dve.snap(n * D), D)], mv2[:, bass.ds(dve.snap(n * 2), 1)],
                                                    rstd[:, bass.ds(n, 1)], ALU.subtract, ALU.mult)
                t.then_inc(xn_ready, 1)

            mv2 = mv[:, :, :].rearrange("p n c -> p (n c)")
            dve.drain()
            layer_norm_stats()
            dve.wait_ge(ln_std, 3)
            nc.vector.reciprocal(rstd[:, :], rstd[:, :])
            dve.drain()
            feed_context(0)
            dve.wait_ge(vr_zeroed, 1)
            dve.wait_ge(c_kv_done, 1)
            nc.vector.tensor_copy(Vh[:, :, 0, :, 0:HD], bank[2][:, :].rearrange("p (b h d) -> p b h d", b=B, h=H))\
                .then_inc(c_v_kept, 1)
            nc.vector.tensor_copy(Vh[0:K1, :, 1, :, 0:HD], bank[3][0:K1, :].rearrange("p (b h d) -> p b h d", b=B, h=H))\
                .then_inc(c_v_kept, 1)
            feed_context(1)
            feed_context(2)
            dve.wait_ge(av_done, 2)
            max_start(TB * 2, 2)
            max_rest()
            max_end(True)
            with dve.Fori(0, B, 1) as b:
                with dve.If(b < B - 1):
                    max_start(TB * 2, 2)
                attend(b, TB, 2)
                max_rest()
                with dve.If(b < B - 1):
                    max_end()
                normalise_out(TB, None)
                with dve.If(b < B - 3):
                    feed_context((b + 3) % B)
                add_out(b, gates[:, 1:2])

            dve.drain()
            layer_norm_stats()
            dve.wait_ge(ln_std, 4)
            nc.vector.reciprocal(rstd[:, :], rstd[:, :])
            dve.drain()
            for n in range(NT):
                t = normalise(rXn[:, n, :], n)
            t.then_inc(rn_ready, 1)
            dve.wait_ge(d_loaded, 16 * 14)
            dve.wait_ge(r_logits, 1)

            def over_experts(v):
                return v.rearrange("p (n o) -> p n o", o=1).broadcast_to([P, NT, E])

            nc.vector.tensor_tensor(lg, bank[4][:, 0:NT * E].rearrange("p (n e) -> p n e", n=NT),
                                    rbb.rearrange("p (o e) -> p o e", o=1).broadcast_to([P, NT, E]), ALU.add)
            dve.drain()
            nc.vector.tensor_reduce(rsum, lg, AX.X, ALU.max)
            dve.drain()
            nc.vector.tensor_tensor(lg, lg, over_experts(rsum), ALU.subtract).then_inc(r_shift, 1)
            dve.wait_ge(d_consts, 5)
            dve.wait_ge(r_exp, 1)
            nc.vector.tensor_reduce(rsum, pr, AX.X, ALU.add)
            dve.drain()
            nc.vector.reciprocal(rsum, rsum)
            dve.drain()
            nc.vector.tensor_tensor(pr, pr, over_experts(rsum), ALU.mult)
            dve.drain()
            for d in range(1, E):
                nc.vector.tensor_tensor(cmp[:, :, 0:E - d], pr[:, :, d:E], pr[:, :, 0:E - d], ALU.is_gt)
                dve.drain()
                nc.vector.tensor_tensor(rank[:, :, 0:E - d], rank[:, :, 0:E - d], cmp[:, :, 0:E - d], ALU.add)
                dve.drain()
                nc.vector.tensor_tensor(rank[:, :, d:E], rank[:, :, d:E], cmp[:, :, 0:E - d], ALU.subtract)
                dve.drain()
            nc.vector.tensor_scalar(memb.rearrange("p t (b e) -> p b t e", b=B), rank.rearrange("p (b t) e -> p b t e", b=B),
                                    2.0, None, ALU.is_lt)
            nc.vector.scalar_tensor_tensor(out=wgt, in0=rank, scalar=2.0, in1=pr, op0=ALU.is_lt, op1=ALU.mult)\
                .then_inc(r_memb, 1)
            dve.drain()
            parts = info.rearrange("p (n e) c -> p n e c", n=NT)
            nc.vector.tensor_copy(parts[:, :, :, 2], wgt)
            dve.drain()
            nc.vector.tensor_tensor(pr, wgt, parts[:, :, :, 2], ALU.subtract)
            dve.drain()
            nc.vector.tensor_copy(parts[:, :, :, 3], pr)
            dve.drain()
            nc.vector.tensor_tensor(parts[:, :, :, 4], pr, parts[:, :, :, 3], ALU.subtract).then_inc(r_info, 1)
            dve.wait_ge(r_pos, 1)
            nc.vector.scalar_tensor_tensor(out=posm, in0=bank[5][:, 0:TB * NG].rearrange("p (t g) -> p t g", t=TB), scalar=1.0,
                                           in1=memb, op0=ALU.add, op1=ALU.mult)
            dve.drain()
            nc.vector.tensor_scalar(posm, posm, 1.0, None, ALU.subtract).then_inc(r_posm, 1)
            dve.wait_ge(r_cnt, 1)
            nc.vector.memset(cnti[:, :], 0)
            nc.vector.tensor_scalar(cntr[0:1, 0, :], bank[6][0:1, 0:NG], float(P), 1.0, ALU.is_gt, ALU.add)
            dve.drain()
            for i in range(2, TB):
                last = i == TB - 1
                nc.vector.scalar_tensor_tensor(out=cnti[:, 0:NG] if last else cntr[0:1, (i - 1) % 2, :], in0=bank[6][0:1, 0:NG],
                                               scalar=float(i * P), in1=cntr[0:1, i % 2, :], op0=ALU.is_gt, op1=ALU.add)
                dve.drain()
            nc.vector.tensor_scalar(cnt[0:1, :], bank[6][0:1, 0:NG], 1.0, None, ALU.max).then_inc(r_counts, 1)
            for r in range(3):
                nc.vector.tensor_copy(xr[:, r * NT:(r + 1) * NT, :], rXn)
                dve.drain()
                if r < 2:
                    nc.vector.tensor_tensor(rXn, rXn, xr[:, r * NT:(r + 1) * NT, :], ALU.subtract)
                    dve.drain()
            dve.sem_inc(xr_ready, 1)
            for b in range(B):
                dve.wait_ge(r_bias_full, b + 1)
                xb = X2[:, b * S:(b + 1) * S]
                nc.vector.scalar_tensor_tensor(out=xb, in0=bank[b][:, :], scalar=gates[:, 3:4], in1=xb,
                                               op0=ALU.mult, op1=ALU.add).then_inc(r_bias_added, 1)

            v_d = counter(dve, "v_d")

            def one_hot(g):
                for t in range(TB):
                    h = nc.vector.tensor_scalar(G[:, t, :], iota16, posm[:, t, bass.ds(g, 1)], None, ALU.is_equal)
                h.then_inc(g_built, 1)

            def one_hot_back(g):
                dve.wait_ge(u_full, dve.snap(v_y) + 1)
                for t in range(TB):
                    at = dve.snap((g % 4) * (2 * TB) + t) if not isinstance(g, int) else (g % 4) * 2 * TB + t
                    h = nc.vector.tensor_scalar(GT[:, t, :], iota16, tokw[:, bass.ds(at, 1)], None, ALU.is_equal)
                h.then_inc(gt_built, 1)

            def expert_prepare(g):
                dve.reg_add(v_d, v_d, 1)
                wait_count(dve, info_full, v_d)
                nc.vector.tensor_copy(isb, bank[3][:, 0:TB * 8].rearrange("p (t c) -> p t c", t=TB)).then_inc(info_kept, 1)
                dve.drain()
                slot = dve.snap(g % 4)
                at = dve.snap(slot * 8)
                at4 = dve.snap(slot * 8 + TB)
                nc.vector.scalar_tensor_tensor(out=tokw[:, bass.ds(at, TB)], in0=isb[:, :, 1], scalar=float(P), in1=isb[:, :, 0],
                                               op0=ALU.mult, op1=ALU.add)
                nc.vector.tensor_tensor(isb[:, :, 5], isb[:, :, 2], isb[:, :, 3], ALU.add)
                dve.drain()
                nc.vector.tensor_tensor(tokw[:, bass.ds(at4, TB)], isb[:, :, 5], isb[:, :, 4], ALU.add).then_inc(tok_ready, 1)
                dve.wait_ge(fill_loaded, dve.snap((dve.snap(v_d) + (B - 1)) * (16 * FILLS)))
                nc.vector.tensor_scalar(mrow[0:1, 1, :], iota[0:1, :], cnt[0:1, bass.ds(g, 1)], NEG, ALU.is_ge, ALU.mult)\
                    .then_inc(mask_ready, 1)
                wait_count(dve, v_full, v_d)
                nc.vector.tensor_tensor(Vh[:, bass.ds(slot, 1), :, :, 0:HD].rearrange("p s k h d -> p (s k) h d"),
                                        bank[3][:, :].rearrange("p (k h d) -> p k h d", k=TB, h=H),
                                        bvb[:, bass.ds(dve.snap(g % E), 1), :].rearrange("p e (h d) -> p e h d", h=H)
                                        .broadcast_to([P, TB, H, HD]), ALU.add).then_inc(v_kept, 1)
                dve.drain()

            def tiles(g):
                return dve.value_load(cnti[0:1, bass.ds(g, 1)], min_val=0, max_val=TB)

            dve.drain()
            one_hot(0)
            for g in range(3):
                expert_prepare(g)
                one_hot(g + 1)
            one_hot_back(0)
            tn = tiles(0)
            max_start(tn * tn, tn)
            max_rest()
            max_end()
            with dve.Fori(0, NG, 1) as g:
                tc = tiles(g)
                tn = tiles(g + 1)
                slot = dve.snap(g % 4)
                weight = dve.snap(slot * 8 + TB)
                max_start(tn * tn, tn)
                for v in range(1, TB + 1):
                    with dve.If(tc == v):
                        attend(slot, v, v)
                        max_rest()
                        with dve.If(g < NG - 1):
                            max_end()
                        normalise_out(v, weight)
                with dve.If(g < NG - 3):
                    expert_prepare((g + 3) % NG)
                with dve.If(g < NG - 4):
                    one_hot((g + 4) % NG)
                add_out(g // E, gates[:, 3:4])
                with dve.If(g < NG - 1):
                    one_hot_back((g + 1) % NG)
                dve.nop()


_INS = ['x', 'ctx_768', 'g_xattn', 'g_ffn', 'L0_xattn_Wq', 'L0_xattn_bq', 'L0_xattn_Wk', 'L0_xattn_bk', 'L0_xattn_Wv',
        'L0_xattn_bv', 'L0_ffn_w_gate', 'L0_ffn_w_up', 'L0_ffn_w_down', 'L1_xattn_w_q', 'L1_xattn_b_q', 'L1_xattn_w_k',
        'L1_xattn_b_k', 'L1_xattn_w_v', 'L1_xattn_b_v', 'L1_xattn_w_o', 'L1_xattn_b_o', 'L1_ffn_router_w',
        'L1_ffn_router_b', 'L1_ffn_wq', 'L1_ffn_bq', 'L1_ffn_wk', 'L1_ffn_bk', 'L1_ffn_wv', 'L1_ffn_bv', 'L1_ffn_wo',
        'L1_ffn_bo']


def kernel(**inputs):
    import numpy as _np
    import concourse.bacc as _bacc
    from concourse.bass_utils import run_bass_kernel_spmd as _run

    nc = _bacc.Bacc("TRN2", target_bir_lowering=False, num_devices=1)
    arrays, args = {}, []
    for name in _INS:
        a = _np.ascontiguousarray(inputs[name])
        arrays[f"in_{name}_dram"] = a
        args.append(nc.dram_tensor(f"in_{name}_dram", a.shape, mybir.dt.from_np(a.dtype), kind="ExternalInput").ap())
    args.append(nc.dram_tensor("out_0_dram", inputs["x"].shape, F32, kind="ExternalOutput").ap())
    build(nc, *args)
    r = _run(nc, [arrays], core_ids=[0])
    return r.results[0]["out_0_dram"]
```

```python
from contextlib import ExitStack

import concourse.bass as bass
from concourse import mybir

F32 = mybir.dt.float32
BF16 = mybir.dt.bfloat16
I32 = mybir.dt.int32
ALU = mybir.AluOpType
ACT = mybir.ActivationFunctionType
AX = mybir.AxisListType
ABSMAX = bass.bass_isa.ReduceOp.absmax

P = 128
ROUND = 1.5 * 2.0**23
Q16 = 32767.0
LN_EPS = 1e-5
NEG = -1e9


def build(nc, x, ctx_768, g_xattn, g_ffn, a_Wq, a_bq, a_Wk, a_bk, a_Wv, a_bv, w_gate, w_up, w_down,
          c_wq, c_bq, c_wk, c_bk, c_wv, c_bv, c_wo, c_bo, router_w, router_b,
          e_wq, e_bq, e_wk, e_bk, e_wv, e_bv, e_wo, e_bo, out):
    B, S, D = x.shape
    _, K, C = ctx_768.shape
    F = w_gate.shape[0]
    E = router_w.shape[1]
    NT = B * S // P
    TB = S // P
    FC = F // P
    K1 = K - P
    CR = B * K
    CT = (CR + P - 1) // P
    CL = CR - (CT - 1) * P
    NBLK = D // 32
    SCALE_A = float(D) ** -0.5
    H, HD = 16, D // 16
    NG = B * E
    SCALE_C, SCALE_E = float(HD) ** -0.5, 0.5
    RING = 3
    QROWS, KROWS = (0, 0, 1, 1, 0, 2), (0, 1, 0, 1, 2, 0)
    MASK = len(QROWS) * HD
    MAXR = MASK + 1
    VW = HD + 1
    FILLS = 14

    with ExitStack() as ctx:
        def sb(name, shape, dt=F32):
            return ctx.enter_context(nc.sbuf_tensor(name, shape, dt))

        def sem(name):
            return ctx.enter_context(nc.semaphore(name))

        X = sb("X", [P, NT, D])
        ident = sb("ident", [P, P])
        ones = sb("ones", [P, P])
        eps = sb("eps", [P, 1])
        rounder = sb("rounder", [P, 1])
        gates = sb("gates", [P, 4])
        graw = sb("graw", [P, 4])
        stats = sb("stats", [P, NT, 6])
        mv = sb("mv", [P, NT, 2])
        rstd = sb("rstd", [P, NT])
        ctxT = sb("ctxT", [P, CR])
        bank = [ctx.enter_context(nc.psum_tensor(f"bank{i}", [P, 512], F32)) for i in range(8)]

        QS = sb("QS", [P, H * RING * S], BF16)
        KS = sb("KS", [P, H * RING * S], BF16)
        Wraw = sb("Wraw", [P, 2, D])
        cWv = sb("cWv", [P, D])
        cWo = sb("cWo", [P, D])
        cBo = sb("cBo", [1, D])
        cBq = sb("cBq", [P, 2])
        ARENA = 24 * 1024
        arena = sb("arena", [P, ARENA])
        top = [0]

        def carve(*shape):
            n = 1
            for d in shape:
                n *= d
            a = top[0]
            top[0] += n
            assert top[0] <= ARENA, top[0]
            v = arena[:, a:a + n]
            if len(shape) == 2:
                v = v.rearrange("p (a b) -> p a b", a=shape[0])
            elif len(shape) == 3:
                v = v.rearrange("p (a b c) -> p a b c", a=shape[0], b=shape[1])
            return v

        W3 = carve(3 * FC, D)
        wmax = carve(3 * FC * NBLK)
        winv = carve(3 * FC * NBLK)
        gateT = carve(F)
        upT = carve(F)
        downT = carve(FC, D)
        top_a = top[0]
        ctx_rows = carve(CT, C)
        aWq = carve(D)
        aWk = carve(D)
        aWv = carve(D)
        aBq = carve(1)
        aKT = carve(CR)
        aV = carve(B, 2, D)
        aXn = [carve(TB, D) for _ in range(2)]
        aXT = [carve(S) for _ in range(2)]
        aQT = [carve(S) for _ in range(2)]
        aP = [carve(TB, K) for _ in range(2)]
        aPT = [carve(2, S) for _ in range(2)]
        aMax = carve(B, TB)
        aSum = carve(B, TB)
        aInv = carve(B, TB)
        top[0] = top_a
        fXn = carve(NT, D)
        fXT = carve(NT * P)
        fG = carve(FC, NT * P)
        fU = carve(FC, NT * P)
        fS = [carve(NT * P), carve(NT * P), fXn.rearrange("p n d -> p (n d)")]
        fpart = carve(2 * FC * B)
        fmax = carve(32)
        fq = carve(16)

        top[0] = 0

        def carve16(*shape):
            n = 1
            for d in shape:
                n *= d
            v = carve(n // 2).bitcast(BF16)
            if len(shape) == 2:
                return v.rearrange("p (a b) -> p a b", a=shape[0])
            return v.rearrange("p (a b c) -> p a b c", a=shape[0], b=shape[1])

        Vr = carve(4 * TB * H * VW)
        V4 = [carve(TB, 4, VW) for _ in range(2)]
        PB = [carve(4 * S) for _ in range(2)]
        Osb = carve(4, S)
        ON = carve(TB, D)
        Usb = carve(S)
        xT = carve(S)
        qf = carve(S)
        kf = carve(CR)
        qp = carve16(3, S)
        kp = carve16(3, CR)
        mrun = carve(TB * H)
        mall = carve(TB, H)
        mres = carve(TB, H)
        nm = carve16(TB, 3, H)
        nmS = carve16(2, S)
        rinv = carve(TB, H)
        identb = carve16(1, P)
        zrow = carve16(2, S)
        mrow = carve16(2, S)
        iota = carve(S)
        iota16 = carve(S // 2).bitcast(mybir.dt.float16)
        xr = carve16(3 * NT, D)
        G = carve16(TB, S)
        GT = carve(TB, S)
        Wqk = carve(2, D)
        Wv = carve(E, D)
        lXn = Wv
        Wo = carve(E, D)
        bvb = carve(E, D)
        bqk = carve(2, E)
        tokw = carve(4 * 2 * TB)
        isb = carve(TB, 8)
        rw = carve(E)
        rbb = carve(E)
        memb = carve16(TB, NG)
        posm = carve(TB, NG)
        info = carve16(NT * E, 8)
        ebo = carve(D)
        cnt = carve(NG)
        lg, pr, rank, cmp, wgt = (Osb[:, 0, i * NT * E:(i + 1) * NT * E].rearrange("p (n e) -> p n e", n=NT) for i in range(5))
        rsum = Osb[:, 1, 0:NT]
        cntr = Osb[:, 1, P:P + 2 * NG].rearrange("p (a g) -> p a g", a=2)
        onesb = Osb[:, 2, 0:P].bitcast(BF16).rearrange("p (a b) -> p a b", a=2)
        trib = Osb[:, 3, 0:P].bitcast(BF16).rearrange("p (a b) -> p a b", a=2)
        rXn = GT.rearrange("p t s -> p (t s)").rearrange("p (n d) -> p n d", d=D)
        rXT = PB[0]
        wTs = [PB[1][:, b * S:(b + 1) * S] for b in range(B)]
        pair, pair_v = (Osb[0:1, i, S // 2:S].rearrange("p (a b) -> p a b", a=NG) for i in (1, 2))
        key, rk, ord_f, til_f = (Osb[0:1, 1, P + (2 + i) * NG:P + (3 + i) * NG] for i in range(4))
        cnti = sb("cnti", [1, 2 * NG], I32)
        order = sb("order", [1, 2 * NG], I32)

        x_loaded = [sem(f"x_loaded{b}") for b in range(B)]
        ctx_loaded = sem("ctx_loaded")
        aw_loaded = sem("aw_loaded")
        g_loaded = sem("g_loaded")
        w3_loaded = sem("w3_loaded")
        consts_ready = sem("consts_ready")
        gates_ready = sem("gates_ready")
        out_stored = sem("out_stored")
        ln_var = sem("ln_var")
        ln_std = sem("ln_std")
        actx_turned = sem("actx_turned")
        actx_ready = sem("actx_ready")
        akv_done = sem("akv_done")
        ak_ready = sem("ak_ready")
        av_ready = sem("av_ready")
        axn_ready = sem("axn_ready")
        axt_done = sem("axt_done")
        axt_ready = sem("axt_ready")
        aq_done = sem("aq_done")
        aq_ready = sem("aq_ready")
        as_done = sem("as_done")
        amax_ready = sem("amax_ready")
        ap_ready = sem("ap_ready")
        apt_done = sem("apt_done")
        apt_ready = sem("apt_ready")
        ao_done = sem("ao_done")
        ax_updated = sem("ax_updated")
        w3_quant = sem("w3_quant")
        w3_turned = sem("w3_turned")
        w3_ready = sem("w3_ready")
        fmax_part = sem("fmax_part")
        fmax_all = sem("fmax_all")
        fxq_ready = sem("fxq_ready")
        fxt_done = sem("fxt_done")
        fxt_ready = sem("fxt_ready")
        fmm_done = sem("fmm_done")
        fmm_kept = sem("fmm_kept")
        fmm_max = sem("fmm_max")
        fq_ready = sem("fq_ready")
        fg_rounded = sem("fg_rounded")
        fu_rounded = sem("fu_rounded")
        fh_rounded = sem("fh_rounded")
        fo_rounded = sem("fo_rounded")
        fgq_ready = sem("fgq_ready")
        fsig_ready = sem("fsig_ready")
        fo_ready = sem("fo_ready")
        fd_done = sem("fd_done")
        fx_updated = sem("fx_updated")

        c_loaded = sem("c_loaded")
        qk_zeroed = sem("qk_zeroed")
        ring_ready = sem("ring_ready")
        c_kv_done = sem("c_kv_done")
        c_k_kept = sem("c_k_kept")
        c_v_kept = sem("c_v_kept")
        c_k_split = sem("c_k_split")
        c_mask = sem("c_mask")
        d_loaded = sem("d_loaded")
        d_consts = sem("d_consts")
        xn_ready = sem("xn_ready")
        xt_full = sem("xt_full")
        xt_kept = sem("xt_kept")
        q_full = sem("q_full")
        q_kept = sem("q_kept")
        k_full = sem("k_full")
        k_kept = sem("k_kept")
        v_full = sem("v_full")
        v_kept = sem("v_kept")
        info_full = sem("info_full")
        info_kept = sem("info_kept")
        split_ready = sem("split_ready")
        fill_loaded = sem("fill_loaded")
        w_loaded = sem("w_loaded")
        g_built = sem("g_built")
        gt_built = sem("gt_built")
        m_full = sem("m_full")
        m_free = sem("m_free")
        nm_split = sem("nm_split")
        nmt_full = sem("nmt_full")
        nms_full = sem("nms_full")
        nm_loaded = sem("nm_loaded")
        s_full = sem("s_full")
        s_free = sem("s_free")
        av_done = sem("av_done")
        o_free = sem("o_free")
        v4_full = sem("v4_full")
        t_full = sem("t_full")
        t_free = sem("t_free")
        u_full = sem("u_full")
        u_kept = sem("u_kept")
        y_full = sem("y_full")
        x_added = sem("x_added")
        rn_ready = sem("rn_ready")
        mask_ready = sem("mask_ready")
        w_placed = sem("w_placed")
        rx_turned = sem("rx_turned")
        rx_kept = sem("rx_kept")
        r_logits = sem("r_logits")
        r_shift = sem("r_shift")
        r_exp = sem("r_exp")
        r_memb = sem("r_memb")
        r_pos = sem("r_pos")
        r_cnt = sem("r_cnt")
        r_counts = sem("r_counts")
        r_info = sem("r_info")
        r_wt = sem("r_wt")
        r_wt_kept = sem("r_wt_kept")
        r_bias_full = sem("r_bias_full")
        r_bias_added = sem("r_bias_added")
        vr_zeroed = sem("vr_zeroed")
        xr_ready = sem("xr_ready")

        x_v = x.rearrange("b (n p) d -> p (b n) d", p=P)
        out_v = out.rearrange("b (n p) d -> p (b n) d", p=P)
        ctx_v = ctx_768.rearrange("b k c -> (b k) c")

        def column(v):
            return v.rearrange("(d o) -> d o", o=1)

        def row(v):
            return v.rearrange("(o d) -> o d", o=1)

        def by_feature(v):
            return v.rearrange("(h d o) -> d h o", d=HD, o=1)

        QS3 = QS[:, :].rearrange("p (h s) -> p h s", h=H)
        KS3 = KS[:, :].rearrange("p (h s) -> p h s", h=H)
        HS = RING * S
        s_bank = [bank[i] for i in (0, 1, 6, 7)]
        SB = len(s_bank)
        X2 = X[:, :, :].rearrange("p n d -> p (n d)")

        def shape_of(tq):
            hp = {1: 4, 2: 2, 3: 1, 4: 1}[tq]
            blocks = 4 if tq == 1 else 2
            return hp, 4 // hp, P * tq, blocks, 4 // blocks

        def counter(eng, name, start=0):
            r = eng.alloc_register(name)
            eng.reg_mov(r, start)
            return r

        def wait_count(eng, s, reg, plus=0):
            eng.wait_ge(s, eng.snap(reg) + plus if plus else reg)

        block = ctx.enter_context(nc.Block())

        @block.sync
        def _(sp):
            for b in range(B):
                sp.dma_start(X[:, b * TB:(b + 1) * TB, :], x_v[:, b * TB:(b + 1) * TB, :]).then_inc(x_loaded[b], 16)
            sp.dma_start(W3[:, 0:FC, :], w_gate.rearrange("(c p) i -> p c i", p=P)).then_inc(w3_loaded, 16)
            sp.dma_start(W3[:, FC:2 * FC, :], w_up.rearrange("(c p) i -> p c i", p=P)).then_inc(w3_loaded, 16)
            sp.dma_start(W3[:, 2 * FC:3 * FC, :], w_down.rearrange("p (c i) -> p c i", c=FC)).then_inc(w3_loaded, 16)
            for dst, src in ((Wraw[:, 0, :], c_wq), (Wraw[0:C, 1, :], c_wk), (Wraw[C:C + 1, 1, :], row(c_bk)), (cWv[0:C, :], c_wv),
                             (cWv[C:C + 1, :], row(c_bv)), (cWo[:, :], c_wo), (cBo[:, :], row(c_bo)),
                             ):
                sp.dma_start(dst, src).then_inc(c_loaded, 16)
            sp.dma_start(cBq[:, 0:1], by_feature(c_bq), allow_slow_non_contiguous=True).then_inc(c_loaded, 16)
            sp.wait_ge(ring_ready, 4)
            sp.wait_ge(fx_updated, B)
            one = zrow[0:1, 1:2, :]
            for i in range(RING):
                sp.dma_start(QS3[MASK:MAXR, :, i * S:(i + 1) * S], one.broadcast_to([1, H, S])).then_inc(qk_zeroed, 16)
                for r in range(3):
                    sp.dma_start(KS3[MAXR + r:MAXR + r + 1, :, i * S:(i + 1) * S], one.broadcast_to([1, H, S]))\
                        .then_inc(qk_zeroed, 16)
            sp.wait_ge(qk_zeroed, 16 * 4 * RING)

            def fill(slot, keys, mask):
                for i, (a, b) in enumerate(zip(QROWS, KROWS)):
                    sp.dma_start(QS3[i * HD:(i + 1) * HD, :, bass.ds(slot, S)], qp[:, a, :]).then_inc(fill_loaded, 16)
                    w, src = keys(b)
                    sp.dma_start(KS3[i * HD:(i + 1) * HD, :, bass.ds(slot, w)], src).then_inc(fill_loaded, 16)
                sp.dma_start(QS3[MAXR:MAXR + 3, :, bass.ds(slot, S)], zrow[0:3, 0:1, :].broadcast_to([3, H, S]))\
                    .then_inc(fill_loaded, 16)
                sp.dma_start(KS3[MASK:MAXR, :, bass.ds(slot, S)], mask).then_inc(fill_loaded, 16)

            def maxima(slot):
                sp.dma_start(QS3[MAXR:MAXR + 3, :, bass.ds(slot, S)],
                             nmS[0:3 * H, 0, :]).then_inc(nm_loaded, 16)

            n_split = counter(sp, "n_split")
            n_nms = counter(sp, "n_nms")

            def context_fill(b):
                sp.reg_add(n_split, n_split, 1)
                wait_count(sp, split_ready, n_split)
                sp.wait_ge(c_k_split, 1)
                sp.wait_ge(c_mask, 1)
                fill(sp.snap((b * S) % HS), lambda n: (K, kp[:, n, bass.ds(b * K, K)]),
                     mrow[0:1, 0:1, :].broadcast_to([1, H, S]))

            def send_maxima(g):
                sp.reg_add(n_nms, n_nms, 1)
                wait_count(sp, nms_full, n_nms)
                maxima(sp.snap((g * S) % HS))

            for b in range(2):
                context_fill(b)
            send_maxima(0)
            context_fill(2)
            with sp.Fori(0, B, 1) as b:
                with sp.If(b < B - 1):
                    send_maxima(b + 1)
                with sp.If(b < B - 3):
                    context_fill((b + 3) % B)
                sp.nop()

            for dst, src in ((Wv, e_wv.rearrange("e d h -> d e h")), (Wo, e_wo.rearrange("e d h -> d e h")),
                             (rw, router_w), (rbb, row(router_b).partition_broadcast(P)),
                             (bvb.rearrange("p e d -> p (e d)"), e_bv.rearrange("(o e) d -> o (e d)", o=1).partition_broadcast(P)),
                             (ebo[0:E, :], e_bo)):
                sp.dma_start(dst, src).then_inc(d_loaded, 16)
            for e in range(E):
                sp.dma_start(bqk[:, 0, e:e + 1], by_feature(e_bq[e, :]), allow_slow_non_contiguous=True).then_inc(d_loaded, 16)
                sp.dma_start(bqk[:, 1, e:e + 1], by_feature(e_bk[e, :]), allow_slow_non_contiguous=True).then_inc(d_loaded, 16)
            n_k = counter(sp, "n_k")

            sp.wait_ge(r_counts, 1)

            def expert_at(g):
                return sp.snap(sp.value_load(order[0:1, bass.ds(g, 1)], min_val=0, max_val=NG - 1) % E)

            def load_qk(e):
                sp.dma_start(Wraw[:, 0, :], e_wq[bass.ds(e, 1), :, :].rearrange("e d h -> (e d) h")).then_inc(w_loaded, 16)
                sp.dma_start(Wraw[:, 1, :], e_wk[bass.ds(e, 1), :, :].rearrange("e d h -> (e d) h")).then_inc(w_loaded, 16)

            def expert_fill(g):
                sp.reg_add(n_split, n_split, 1)
                wait_count(sp, split_ready, n_split)
                wait_count(sp, mask_ready, n_k)
                fill(sp.snap((g * S) % HS), lambda n: (S, kp[:, n, 0:S]),
                     mrow[0:1, 1:2, :].broadcast_to([1, H, S]))

            load_qk(expert_at(0))
            for g in range(3):
                if g == 2:
                    send_maxima(0)
                e = expert_at(g + 1)
                sp.reg_add(n_k, n_k, 1)
                wait_count(sp, w_placed, n_k, 1)
                load_qk(e)
                expert_fill(g)
            with sp.Fori(0, NG, 1) as g:
                send_maxima(g + 1)
                with sp.If(g < NG - 3):
                    e = expert_at(g + 4)
                    sp.reg_add(n_k, n_k, 1)
                    wait_count(sp, w_placed, n_k, 1)
                    load_qk(e)
                    expert_fill((g + 3) % NG)
                sp.nop()
                with sp.If(g == NG - 3):
                    sp.wait_ge(fill_loaded, 16 * FILLS * (B + NG))
                    sp.sem_inc(fill_loaded, 16 * FILLS)
                sp.nop()
            sp.wait_ge(x_added, 1 + B + NG)
            sp.wait_ge(nm_loaded, 16 * (B + NG + 1))
            sp.wait_ge(w_loaded, 32 * (NG + 1))
            sp.dma_start(out_v, X[:, :, :]).then_inc(out_stored, 16)
            sp.wait_ge(out_stored, 16)

        @block.gpsimd
        def _(pool):
            nc.gpsimd.memset(ones[:, :], 1.0).then_inc(consts_ready, 1)
            nc.gpsimd.memset(rounder[:, :], ROUND)
            nc.gpsimd.memset(eps[:, :], LN_EPS).then_inc(consts_ready, 1)
            pool.drain()
            nc.gpsimd.memset(ctxT[96:97, :], 1.0).then_inc(consts_ready, 1)
            pool.drain()
            nc.gpsimd.memset(ident[:, :], 0.0)
            pool.drain()
            nc.gpsimd.affine_select(out=ident[:, :], in_=ident[:, :], compare_op=ALU.not_equal, fill=1.0,
                                    base=0, pattern=[[-1, P]], channel_multiplier=1).then_inc(consts_ready, 1)
            pool.drain()
            nc.gpsimd.memset(QS[:, :].bitcast(F32), 0.0).then_inc(ring_ready, 1)
            pool.drain()
            nc.gpsimd.memset(KS[:, :].bitcast(F32), 0.0).then_inc(ring_ready, 1)
            for i in range(5):
                pool.wait_ge(fmax_part, i + 1)
                nc.gpsimd.partition_all_reduce(fmax[:, 16 + i:17 + i], fmax[:, i:i + 1], P, ABSMAX)\
                    .then_inc(fmax_all, 1)
            pool.wait_ge(fx_updated, B)
            nc.gpsimd.memset(zrow[:, 0, :], 0.0).then_inc(ring_ready, 1)
            pool.drain()
            nc.gpsimd.memset(zrow[:, 1, :], 1.0).then_inc(ring_ready, 1)
            pool.drain()
            nc.gpsimd.memset(mrow[0:1, 0, 0:K], 0.0)
            pool.drain()
            nc.gpsimd.memset(mrow[0:1, 0, K:S], NEG).then_inc(c_mask, 1)
            pool.drain()
            nc.gpsimd.memset(Vr, 0.0)
            pool.drain()
            nc.gpsimd.memset(Vr.rearrange("p (n w) -> p n w", w=VW)[:, :, HD:VW], 1.0).then_inc(vr_zeroed, 1)
            pool.drain()
            nc.gpsimd.tensor_copy(identb[:, 0, :], ident[:, :])
            pool.drain()

            def split(v, p):
                nc.gpsimd.tensor_tensor(v, v, p[:, 0, :], ALU.subtract)
                pool.drain()
                nc.gpsimd.tensor_copy(p[:, 1, :], v)
                pool.drain()
                return nc.gpsimd.tensor_tensor(p[:, 2, :], v, p[:, 1, :], ALU.subtract)

            def place_weights(rows):
                for i, n in enumerate(rows):
                    t = nc.gpsimd.tensor_copy(Wqk[0:n, i, :].rearrange("p (d h) -> p d h", d=HD),
                                              Wraw[0:n, i, :].rearrange("p (h d) -> p d h", d=HD))
                t.then_inc(w_placed, 1)
                pool.drain()

            pool.wait_ge(c_loaded, 16 * 8)
            place_weights((D, C + 1))
            n_q = counter(pool, "n_q", 3)

            def split_queries():
                pool.reg_add(n_q, n_q, 1)
                wait_count(pool, q_kept, n_q)
                return split(qf, qp)

            split_queries().then_inc(split_ready, 1)
            pool.reg_add(n_q, n_q, 3)

            pool.wait_ge(x_added, 1 + B)
            pool.drain()
            nc.gpsimd.iota(iota, pattern=[[1, S]], base=0, channel_multiplier=0, allow_small_or_imprecise_dtypes=True)\
                .then_inc(d_consts, 1)
            pool.drain()
            nc.gpsimd.tensor_copy(iota16, iota)
            pool.drain()
            nc.gpsimd.memset(onesb[:, 0, :], 1.0).then_inc(d_consts, 1)
            pool.drain()
            nc.gpsimd.affine_select(out=trib[:, 0, :], in_=onesb[:, 0, :], compare_op=ALU.is_gt, fill=0.0, base=0,
                                    pattern=[[1, P]], channel_multiplier=-1).then_inc(d_consts, 1)
            pool.drain()
            nc.gpsimd.iota(rank, pattern=[[0, NT], [1, E]], base=0, channel_multiplier=0,
                           allow_small_or_imprecise_dtypes=True).then_inc(d_consts, 1)
            pool.drain()
            nc.gpsimd.memset(info, 0.0)
            pool.drain()
            nc.gpsimd.iota(info[:, :, 0], pattern=[[0, NT * E]], base=0, channel_multiplier=1,
                           allow_small_or_imprecise_dtypes=True)
            pool.drain()
            nc.gpsimd.iota(info.rearrange("p (b t e) c -> p b t e c", b=B, t=TB)[:, :, :, :, 1], pattern=[[0, B], [1, TB], [0, E]],
                           base=0, channel_multiplier=0, allow_small_or_imprecise_dtypes=True).then_inc(d_consts, 1)
            pool.drain()
            def split_group():
                split_queries()
                wait_count(pool, k_kept, n_w)
                split(kf[:, 0:S], kp[:, :, 0:S]).then_inc(split_ready, 1)
                pool.drain()

            n_w = counter(pool, "n_w")

            def place_expert(first=False):
                if not first:
                    wait_count(pool, k_full, n_w)
                pool.wait_ge(w_loaded, pool.snap(n_w) * 32 + 32)
                pool.reg_add(n_w, n_w, 1)
                place_weights((D, D))

            place_expert(True)
            for g in range(3):
                place_expert()
            with pool.Fori(0, NG - 3, 1) as g:
                split_group()
                place_expert()

        @block.tensor
        def _(pe):
            pe.wait_ge(consts_ready, 4)

            pe.wait_ge(ctx_loaded, 32)
            for i in range(CT):
                n = P if i < CT - 1 else CL
                t = nc.tensor.transpose(bank[i // 4][0:C, (i % 4) * P:(i % 4) * P + n], ctx_rows[0:n, i, :], ident[0:n, 0:n])
            t.then_inc(actx_turned, 1)
            pe.wait_ge(aw_loaded, 16 * 6)
            pe.wait_ge(actx_ready, 2)
            for i in range(2):
                nc.tensor.matmul(bank[2 + i][:, 0:CR // 2], aWk[0:C + 1, :], ctxT[0:C + 1, i * CR // 2:(i + 1) * CR // 2],
                                 start=True, stop=True)
            for b in range(B):
                nc.tensor.matmul(bank[4][:, b * D:(b + 1) * D], ctxT[0:C + 1, b * K:b * K + P], aWv[0:C + 1, :],
                                 start=True, stop=True)
                t = nc.tensor.matmul(bank[5][0:K1, b * D:(b + 1) * D], ctxT[0:C + 1, b * K + P:(b + 1) * K], aWv[0:C + 1, :],
                                     start=True, stop=True)
            t.then_inc(akv_done, 1)

            def project(b):
                p = b % 2
                pe.wait_ge(axn_ready, b + 1)
                if b >= 2:
                    pe.wait_ge(ax_updated, b - 1)
                for i in range(TB):
                    t = nc.tensor.transpose(bank[p][:, i * P:(i + 1) * P], aXn[p][:, i, :], ident[:, :])
                t.then_inc(axt_done, 1)
                pe.wait_ge(axt_ready, b + 1)
                if b < 2:
                    pe.wait_ge(ak_ready, 2)
                else:
                    pe.wait_ge(aq_ready, b - 1)
                nc.tensor.matmul(bank[2 + p][:, :], aWq, aXT[p], start=True, stop=True).then_inc(aq_done, 1)

            project(0)
            for b in range(B):
                p = b % 2
                pe.wait_ge(aq_ready, b + 1)
                pe.wait_ge(av_ready, 2)
                if b >= 1:
                    pe.wait_ge(ap_ready, b)
                for i in range(TB):
                    t = nc.tensor.matmul(bank[4 + i // 2][:, (i % 2) * 256:(i % 2) * 256 + K], aQT[p][:, i * P:(i + 1) * P],
                                         aKT[:, b * K:(b + 1) * K], start=True, stop=True)
                t.then_inc(as_done, 1)
                if b + 1 < B:
                    project(b + 1)
                pe.wait_ge(ap_ready, b + 1)
                if b >= 1:
                    pe.wait_ge(apt_ready, 2 * b)
                for i in range(TB):
                    nc.tensor.transpose(bank[6][:, i * P:(i + 1) * P], aP[p][:, i, 0:P], ident[:, :])
                    t = nc.tensor.transpose(bank[7][0:K1, i * P:(i + 1) * P], aP[p][:, i, P:K], ident[:, :])
                t.then_inc(apt_done, 1)
                pe.wait_ge(apt_ready, 2 * b + 2)
                for i in range(TB):
                    nc.tensor.matmul(bank[p][:, i * D:(i + 1) * D], aPT[p][:, 0, i * P:(i + 1) * P], aV[:, b, 0, :],
                                     start=True, stop=False)
                    t = nc.tensor.matmul(bank[p][:, i * D:(i + 1) * D], aPT[p][0:K1, 1, i * P:(i + 1) * P],
                                         aV[0:K1, b, 1, :], start=False, stop=True)
                t.then_inc(ao_done, 1)

            pe.wait_ge(w3_quant, 1)
            for m in range(3):
                if m == 2:
                    pe.wait_ge(ax_updated, B)
                    pe.wait_ge(apt_ready, 2 * B)
                for c in range(FC):
                    t = nc.tensor.transpose(bank[(2, 3, 6)[m]][:, c * P:(c + 1) * P], W3[:, m * FC + c, :], ident[:, :])
                t.then_inc(w3_turned, 1)
            for b in range(B):
                pe.wait_ge(fxq_ready, b + 1)
                for i in range(TB):
                    t = nc.tensor.transpose(bank[(0, 1, 4, 5)[b]][:, i * P:(i + 1) * P], fXn[:, b * TB + i, :], ident[:, :])
                t.then_inc(fxt_done, 1)
            pe.wait_ge(w3_ready, 3)
            n = 0
            for w in (gateT, upT):
                for c in range(FC):
                    for b in range(B):
                        if n < B:
                            pe.wait_ge(fxt_ready, n + 1)
                        if n == 0:
                            pe.wait_ge(fxt_ready, B)
                        if n >= 8:
                            pe.wait_ge(fmm_kept, n - 7)
                            pe.wait_ge(fmm_max, n - 7)
                        nc.tensor.matmul(bank[n % 8][:, :], w[:, c * P:(c + 1) * P], fXT[:, b * S:(b + 1) * S],
                                         start=True, stop=True).then_inc(fmm_done, 1)
                        n += 1
            pe.wait_ge(fo_ready, FC)
            pe.wait_ge(fmm_kept, n)
            pe.wait_ge(fmm_max, n)
            for b in range(B):
                for i in range(TB):
                    for c in range(FC):
                        t = nc.tensor.matmul(bank[b][:, i * D:(i + 1) * D], fG[:, c, (b * TB + i) * P:(b * TB + i + 1) * P],
                                             downT[:, c, :], start=(c == 0), stop=(c == FC - 1))
                t.then_inc(fd_done, 1)

            pe.sem_inc(t_full, 1)
            pe.sem_inc(u_full, 1)
            n_s = counter(pe, "n_s")
            n_m = counter(pe, "n_m")
            n_c = counter(pe, "n_c")
            n_t = counter(pe, "n_t")
            n_g = counter(pe, "n_g")
            n_b = counter(pe, "n_b")
            n_nm = counter(pe, "n_nm")
            n_x = counter(pe, "n_x")
            left = counter(pe, "left")
            unit = counter(pe, "unit")
            two = counter(pe, "two")
            q_at = counter(pe, "q_at")
            k_at = counter(pe, "k_at")
            k_base = counter(pe, "k_base")

            def max_point():
                u = pe.snap(unit, min_val=0, max_val=2 * TB)
                w = pe.snap(two, min_val=0, max_val=1)
                pe.reg_mov(q_at, pe.snap(k_base, min_val=0, max_val=HS) + ((u >> w) * P + (u & w) * (8 * HS)))
                pe.reg_mov(k_at, pe.snap(k_base, min_val=0, max_val=HS) + (u & w) * (8 * HS))

            def max_start(g, units, pairs):
                pe.reg_add(left, left, units)
                pe.reg_mov(two, pairs - 1)
                pe.reg_mov(unit, 0)
                pe.reg_mov(k_base, pe.snap((g * S) % HS))
                max_point()

            def max_at(wide):
                top = 2 * S + 3 * P + (8 * HS if wide else 0)
                return (pe.snap(q_at, min_val=0, max_val=top), pe.snap(k_at, min_val=0, max_val=top - 3 * P), pe.snap(n_m))

            def max_bank(c, at, wide):
                q, k, before = at
                pe.wait_ge(m_free, before + (c + 1))
                heads = [c] if wide else [2 * c, 2 * c + 1]
                n = S // len(heads)
                for j, h in enumerate(heads):
                    t = nc.tensor.matmul(bank[2 + c % 2][:, j * n:(j + 1) * n], QS[:, bass.ds(q + h * HS, P)],
                                         KS[:, bass.ds(k + h * HS, n)], start=True, stop=True)
                t.then_inc(m_full, 1)
                if c == 7:
                    pe.reg_add(n_m, n_m, 8)
                    pe.reg_add(unit, unit, 1)
                    pe.reg_sub(left, left, 1)
                    max_point()

            def max_units(wide):
                with pe.Fori(0, pe.snap(left), 1):
                    at = max_at(wide)
                    for c in range(8):
                        max_bank(c, at, wide)

            def max_rest():
                with pe.If(pe.snap(left) > 0):
                    with pe.If(pe.snap(two) > 0):
                        max_units(True)
                    with pe.Else():
                        max_units(False)
                    pe.nop()
                pe.nop()

            def attend(g, tq, tk, modes):
                hp, banks, N, blocks, loops = shape_of(tq)
                slot = pe.snap((g * S) % HS)

                def one_pass(it):
                    at = pe.snap(slot + it * (blocks * 4 * HS), min_val=0, max_val=15 * HS)
                    steps = [(m, i) for m in range(blocks * tk) for i in range(banks)]
                    before = pe.snap(n_s)
                    before_c = pe.snap(n_c)
                    groups = pe.snap(n_g)

                    def scores(x):
                        m, i = steps[x]
                        cp, kt = m // tk, m % tk
                        if x % 2 == 0:
                            pe.wait_ge(s_free, before + (x + 2))
                        if x == SB - 1:
                            pe.wait_ge(x_added, groups + 1)
                        for jj in range(hp):
                            h = 4 * cp + i * hp + jj
                            t = nc.tensor.matmul(s_bank[x % SB][:, jj * N:(jj + 1) * N], KS[:, bass.ds(at + (h * HS + kt * P), P)],
                                                 QS[:, bass.ds(at + h * HS, N)], start=True, stop=True)
                        t.then_inc(s_full, 1)

                    def av(m):
                        cp, kt = m // tk, m % tk
                        if kt == 0:
                            pe.wait_ge(o_free, before_c + (cp + 1))
                            pe.wait_ge(v4_full, before_c + (cp + 1))
                        pe.wait_ge(s_free, before + ((m + 1) * banks + SB))
                        for j in range(4):
                            t = nc.tensor.matmul(bank[4 + cp % 2][32 * j:32 * j + VW, 0:N], V4[cp % 2][:, kt, j, :],
                                                 PB[m % 2][:, j * N:(j + 1) * N], start=(kt == 0), stop=(kt == tk - 1),
                                                 skip_group_check=True)
                        t.then_inc(av_done, 1)

                    def run(xs, with_max, wide=False):
                        if with_max:
                            unit_at = max_at(wide)
                        for x in xs:
                            m, i = steps[x]
                            scores(x)
                            if with_max:
                                max_bank(x % 8, unit_at, wide)
                            if m and i == min(2, banks - 1):
                                av(m - 1)

                    for x in range(0, len(steps), 8):
                        xs = range(x, min(x + 8, len(steps)))
                        if tq == 1:
                            run(xs, False)
                        else:
                            with pe.If(pe.snap(left) > 0):
                                if len(modes) == 1:
                                    run(xs, True, modes[0])
                                else:
                                    with pe.If(pe.snap(two) > 0):
                                        run(xs, True, True)
                                    with pe.Else():
                                        run(xs, True, False)
                                    pe.nop()
                            with pe.Else():
                                run(xs, False)
                    av(blocks * tk - 1)
                    pe.reg_add(n_s, n_s, len(steps))
                    pe.reg_add(n_c, n_c, blocks)

                if loops == 1:
                    one_pass(0)
                else:
                    with pe.Fori(0, loops, 1) as it:
                        one_pass(it)

            def turn_out(tq):
                pe.wait_ge(o_free, pe.snap(n_c) + 2)
                wait_count(pe, u_kept, n_g, 1)
                wait_count(pe, x_added, n_g, 1)
                for q in range(tq):
                    pe.reg_add(n_t, n_t, 1)
                    wait_count(pe, t_free, n_t)
                    for c in range(4):
                        t = nc.tensor.transpose(bank[6 + q % 2][:, c * P:(c + 1) * P], Osb[:, c, q * P:(q + 1) * P], ident[:, :])
                    t.then_inc(t_full, 1)

            def turn_maxima():
                wait_count(pe, nm_split, n_nm, 1)
                pe.reg_add(n_nm, n_nm, 1)
                for q in range(TB):
                    t = nc.tensor.transpose(bank[0][:, :].bitcast(BF16)[0:3 * H, q * P:(q + 1) * P],
                                            nm[:, q, :, :].rearrange("p r h -> p (r h)"), identb[:, 0, :])
                t.then_inc(nmt_full, 1)

            def ready(n):
                pe.wait_ge(fill_loaded, pe.snap(n * (16 * FILLS)))

            pe.wait_ge(c_loaded, 16 * 8)
            pe.wait_ge(w_placed, 1)
            pe.wait_ge(fx_updated, B)
            pe.wait_ge(vr_zeroed, 1)
            for i in range(2):
                nc.tensor.matmul(bank[i][:, 0:CR // 2], Wqk[0:C + 1, 1, :], ctxT[0:C + 1, i * CR // 2:(i + 1) * CR // 2],
                                 start=True, stop=True)
            for b in range(B):
                nc.tensor.matmul(bank[2][:, b * D:(b + 1) * D], ctxT[0:C + 1, b * K:b * K + P], cWv[0:C + 1, :],
                                 start=True, stop=True)
                t = nc.tensor.matmul(bank[3][0:K1, b * D:(b + 1) * D], ctxT[0:C + 1, b * K + P:(b + 1) * K], cWv[0:C + 1, :],
                                     start=True, stop=True)
            t.then_inc(c_kv_done, 1)
            for i in range(2):
                t = nc.tensor.matmul(bank[4 + i][:, :], zrow[:, 0, 0:P], zrow[:, 0, :], start=True, stop=True)
            t.then_inc(av_done, 2)
            pe.wait_ge(c_v_kept, 2)
            pe.wait_ge(c_k_kept, 4)

            def context_prepare():
                pe.reg_add(n_x, n_x, 1)
                wait_count(pe, xn_ready, n_x)
                for i in range(TB):
                    t = nc.tensor.transpose(bank[2][:, i * P:(i + 1) * P], lXn[:, i, :], ident[:, :])
                t.then_inc(xt_full, 1)
                wait_count(pe, xt_kept, n_x)
                nc.tensor.matmul(bank[1][:, :], Wqk[:, 0, :], xT, start=True, stop=True).then_inc(q_full, 1)

            def finish(g, tq, expert):
                if expert:
                    pe.wait_ge(t_free, pe.snap(n_t) + 2)
                    pe.reg_add(n_e, n_e, 1)
                    wait_count(pe, gt_built, n_e)
                    for q in range(tq):
                        t = nc.tensor.matmul(bank[6][:, :], ON[:, q, :], GT[:, q, :], start=(q == 0), stop=(q == tq - 1))
                else:
                    pe.wait_ge(t_free, pe.snap(n_t) + 2)
                    for q in range(tq):
                        t = nc.tensor.transpose(bank[6][:, q * P:(q + 1) * P], ON[:, q, :], ident[:, :])
                t.then_inc(u_full, 1)

            def project_out(e, expert):
                pe.reg_add(n_g, n_g, 1)
                wait_count(pe, u_kept, n_g, 1)
                for i in range(TB):
                    w = Wo[:, bass.ds(e, 1), :].rearrange("p e d -> p (e d)") if expert else cWo[:, :]
                    t = nc.tensor.matmul(bank[7][:, i * D:(i + 1) * D], Usb[:, i * P:(i + 1) * P], w, start=True, stop=expert)
                    if not expert:
                        t = nc.tensor.matmul(bank[7][:, i * D:(i + 1) * D], ones[0:1, :], cBo[:, :], start=False, stop=True)
                t.then_inc(y_full, 1)

            for b in range(2):
                context_prepare()
                wait_count(pe, q_kept, n_x)
            pe.wait_ge(qk_zeroed, 16 * 4 * RING)
            ready(1)
            max_start(0, TB, 1)
            max_rest()
            pe.wait_ge(m_free, pe.snap(n_m) + 2)
            turn_maxima()
            context_prepare()
            with pe.Fori(0, B, 1) as b:
                with pe.If(b < B - 1):
                    max_start(b + 1, TB, 1)
                    ready(b + 2)
                wait_count(pe, q_kept, n_x)
                pe.wait_ge(nm_loaded, pe.snap(n_b) * 16 + 16)
                pe.reg_add(n_b, n_b, 1)
                attend(b, TB, 2, (False,))
                max_rest()
                turn_out(TB)
                pe.wait_ge(m_free, pe.snap(n_m) + 2)
                with pe.If(b < B - 1):
                    turn_maxima()
                with pe.If(b < B - 3):
                    context_prepare()
                finish(b, TB, False)
                project_out(b, False)

            pe.wait_ge(x_added, 1 + B)
            pe.wait_ge(rn_ready, 1)
            for b in range(B):
                for i in range(TB):
                    t = nc.tensor.transpose(bank[b][:, i * P:(i + 1) * P], rXn[:, b * TB + i, :], ident[:, :])
                t.then_inc(rx_turned, 1)
            pe.wait_ge(d_loaded, 16 * 14)
            for b in range(B):
                pe.wait_ge(rx_kept, b + 1)
                for i in range(TB):
                    n = b * TB + i
                    t = nc.tensor.matmul(bank[4][:, n * E:(n + 1) * E], rXT[:, n * P:(n + 1) * P], rw, start=True, stop=True)
            t.then_inc(r_logits, 1)
            pe.wait_ge(r_memb, 1)
            pe.wait_ge(d_consts, 5)
            for t in range(TB):
                for u in range(t + 1):
                    h = nc.tensor.matmul(bank[5][:, t * NG:(t + 1) * NG], (trib if u == t else onesb)[:, 0, :], memb[:, u, :],
                                         start=(u == 0), stop=(u == t))
            h.then_inc(r_pos, 1)
            for t in range(TB):
                h = nc.tensor.matmul(bank[6][0:1, 0:NG], onesb[:, 0, 0:1], memb[:, t, :], start=(t == 0), stop=(t == TB - 1))
            h.then_inc(r_cnt, 1)
            for n in range(NT):
                t = nc.tensor.transpose(bank[n // 4][0:E, (n % 4) * P:(n % 4 + 1) * P], wgt[:, n, :], ident[:, :])
                if n % 4 == 3:
                    t.then_inc(r_wt, 1)
            pe.wait_ge(r_wt_kept, B)

            def output_biases():
                for b in range(B):
                    if b >= 2:
                        pe.wait_ge(r_bias_added, b - 1)
                    for i in range(TB):
                        t = nc.tensor.matmul(bank[6 + b % 2][:, i * D:(i + 1) * D], wTs[b][0:E, i * P:(i + 1) * P], ebo[0:E, :],
                                             start=True, stop=True)
                    t.then_inc(r_bias_full, 1)

            pe.wait_ge(r_info, 1)
            pe.wait_ge(xr_ready, 1)
            pe.wait_ge(r_counts, 1)
            n_d = counter(pe, "n_d")
            n_e = counter(pe, "n_e")

            def group_at(g):
                return pe.value_load(order[0:1, bass.ds(g, 1)], min_val=0, max_val=NG - 1)

            def expert_prepare(which):
                e = pe.snap(which % E)
                b4 = pe.snap((which // E) * TB)
                pe.reg_add(n_x, n_x, 1)
                pe.reg_add(n_d, n_d, 1)
                wait_count(pe, g_built, n_d)
                for t in range(TB):
                    for r in range(3):
                        h = nc.tensor.matmul(bank[2][:, :], xr[:, bass.ds(pe.snap(b4 + (r * NT + t)), 1), :].rearrange("p n d -> p (n d)"),
                                             G[:, t, :], start=(t == 0 and r == 0), stop=(t == TB - 1 and r == 2))
                h.then_inc(xt_full, 1)
                for k in range(TB):
                    for t in range(TB):
                        h = nc.tensor.matmul(bank[3][:, k * 8:(k + 1) * 8], G[:, t, k * P:(k + 1) * P],
                                             info[:, bass.ds(pe.snap((b4 + t) * E + e), 1), :].rearrange("p n c -> p (n c)"),
                                             start=(t == 0), stop=(t == TB - 1))
                h.then_inc(info_full, 1)
                wait_count(pe, xt_kept, n_x)
                wait_count(pe, w_placed, n_d, 1)
                nc.tensor.matmul(bank[1][:, :], Wqk[:, 0, :], xT, start=True, stop=True).then_inc(q_full, 1)
                nc.tensor.matmul(bank[2][:, :], Wqk[:, 1, :], xT, start=True, stop=True).then_inc(k_full, 1)
                wait_count(pe, info_kept, n_d)
                for k in range(TB):
                    h = nc.tensor.matmul(bank[3][:, k * P:(k + 1) * P], xT[:, k * P:(k + 1) * P],
                                         Wv[:, bass.ds(e, 1), :].rearrange("p e d -> p (e d)"), start=True, stop=True)
                h.then_inc(v_full, 1)

            def prepared():
                wait_count(pe, q_kept, n_x)
                wait_count(pe, k_kept, n_d)
                wait_count(pe, v_kept, n_d)

            def tiles(g):
                return pe.value_load(cnti[0:1, bass.ds(g, 1)], min_val=0, max_val=TB)

            tn = tiles(0)
            first = [group_at(g) for g in range(3)]
            for g in range(2):
                expert_prepare(first[g])
                if g == 0:
                    output_biases()
                prepared()
            pe.wait_ge(r_bias_added, B)
            ready(B + 1)
            max_start(0, tn * ((tn + 1) >> 1), (tn + 1) >> 1)
            max_rest()
            pe.wait_ge(m_free, pe.snap(n_m) + 2)
            turn_maxima()
            expert_prepare(first[2])
            tc = counter(pe, "tc")
            tnext = counter(pe, "tnext")
            pe.reg_mov(tc, tn)
            t1 = tiles(1)
            pe.reg_mov(tnext, t1)
            max_start(1, t1 * ((t1 + 1) >> 1), (t1 + 1) >> 1)
            with pe.Fori(0, NG, 1) as g:
                prepared()
                pe.wait_ge(nm_loaded, pe.snap(n_b) * 16 + 16)
                ready(g + (B + 2))
                pe.reg_add(n_b, n_b, 1)
                for v in range(1, TB + 1):
                    with pe.If(pe.snap(tc) == v):
                        attend(g, v, v, (True,) if v > 2 else (True, False))
                        max_rest()
                        turn_out(v)
                pe.wait_ge(m_free, pe.snap(n_m) + 2)
                turn_maxima()
                with pe.If(g < NG - 3):
                    expert_prepare(group_at((g + 3) % NG))
                for v in range(1, TB + 1):
                    with pe.If(pe.snap(tc) == v):
                        finish(g, v, True)
                t2 = tiles(g + 2)
                max_start(g + 2, t2 * ((t2 + 1) >> 1), (t2 + 1) >> 1)
                pe.reg_mov(tc, tnext)
                pe.reg_mov(tnext, t2)
                e = pe.snap(group_at(g) % E)
                project_out(e, True)

        @block.scalar
        def _(act):
            act.dma_start(ctx_rows[:, 0:CT - 1, :], ctx_v[0:(CT - 1) * P, :].rearrange("(n p) c -> p n c", p=P))\
                .then_inc(ctx_loaded, 16)
            act.dma_start(ctx_rows[0:CL, CT - 1, :], ctx_v[(CT - 1) * P:CR, :]).then_inc(ctx_loaded, 16)
            act.dma_start(graw[:, 0:2], row(g_xattn).partition_broadcast(P)).then_inc(g_loaded, 16)
            act.dma_start(graw[:, 2:4], row(g_ffn).partition_broadcast(P)).then_inc(g_loaded, 16)
            act.dma_start(aWq, a_Wq).then_inc(aw_loaded, 16)
            act.dma_start(aBq, column(a_bq)).then_inc(aw_loaded, 16)
            act.dma_start(aWk[0:C, :], a_Wk).then_inc(aw_loaded, 16)
            act.dma_start(aWk[C:C + 1, :], row(a_bk)).then_inc(aw_loaded, 16)
            act.dma_start(aWv[0:C, :], a_Wv).then_inc(aw_loaded, 16)
            act.dma_start(aWv[C:C + 1, :], row(a_bv)).then_inc(aw_loaded, 16)
            act.wait_ge(g_loaded, 32)
            nc.scalar.activation(gates[:, :], graw[:, :], ACT.Tanh).then_inc(gates_ready, 1)
            act.wait_ge(actx_turned, 1)
            nc.scalar.copy(ctxT[0:C, 0:512], bank[0][0:C, :]).then_inc(actx_ready, 1)
            nc.scalar.copy(ctxT[0:C, 512:CR], bank[1][0:C, 0:CR - 512]).then_inc(actx_ready, 1)
            act.wait_ge(consts_ready, 4)
            act.wait_ge(ln_var, 1)
            nc.scalar.activation(rstd[:, :], mv[:, :, 1], ACT.Sqrt, bias=eps[:, :]).then_inc(ln_std, 1)
            act.wait_ge(akv_done, 1)
            for i in range(2):
                nc.scalar.copy(aKT[:, i * CR // 2:(i + 1) * CR // 2], bank[2 + i][:, 0:CR // 2]).then_inc(ak_ready, 1)

            def project(b):
                p = b % 2
                act.wait_ge(axt_done, b + 1)
                if b >= 2:
                    act.wait_ge(aq_done, b - 1)
                nc.scalar.copy(aXT[p], bank[p][:, :]).then_inc(axt_ready, 1)
                act.wait_ge(aq_done, b + 1)
                if b >= 2:
                    act.wait_ge(as_done, b - 1)
                nc.scalar.activation(aQT[p], bank[2 + p][:, :], ACT.Identity, bias=aBq).then_inc(aq_ready, 1)

            project(0)
            for b in range(B):
                p = b % 2
                if b + 1 < B:
                    project(b + 1)
                act.wait_ge(amax_ready, b + 1)
                if b >= 2:
                    act.wait_ge(apt_done, b - 1)
                for i in range(TB):
                    t = nc.scalar.activation(aP[p][:, i, :], bank[4 + i // 2][:, (i % 2) * 256:(i % 2) * 256 + K], ACT.Exp,
                                             bias=aMax[:, b, i:i + 1], scale=SCALE_A, accum_out=aSum[:, b, i:i + 1])
                t.then_inc(ap_ready, 1)

            for m, dst in enumerate((gateT, upT, downT.rearrange("p a b -> p (a b)"))):
                act.wait_ge(w3_turned, m + 1)
                nc.scalar.copy(dst, bank[(2, 3, 6)[m]][:, 0:F]).then_inc(w3_ready, 1)
            act.wait_ge(ln_var, 2)
            act.wait_ge(axn_ready, B)
            nc.scalar.activation(rstd[:, :], mv[:, :, 1], ACT.Sqrt, bias=eps[:, :]).then_inc(ln_std, 1)
            for b in range(B):
                act.wait_ge(fxt_done, b + 1)
                nc.scalar.copy(fXT[:, b * S:(b + 1) * S], bank[(0, 1, 4, 5)[b]][:, :]).then_inc(fxt_ready, 1)
            n = 0
            for dst in (fG, fU):
                for c in range(FC):
                    for b in range(B):
                        act.wait_ge(fmm_done, n + 1)
                        act.wait_ge(fmm_max, n + 1)
                        nc.scalar.copy(dst[:, c, b * S:(b + 1) * S], bank[n % 8][:, :]).then_inc(fmm_kept, 1)
                        n += 1

            def round_up(v, inverse, done):
                nc.scalar.activation(v, v, ACT.Identity, bias=rounder[:, :], scale=inverse).then_inc(done, 1)

            act.drain()
            act.wait_ge(fq_ready, 1)
            for c in range(1, FC):
                round_up(fG[:, c, :], fq[:, 3:4], fg_rounded)
            for c in range(FC):
                act.wait_ge(fgq_ready, c + 1)
                nc.scalar.activation(fS[c], fG[:, c, :], ACT.Sigmoid)
                act.drain()
                round_up(fS[c], 65536.0, fsig_ready)
            act.wait_ge(fq_ready, 2)
            for c in range(1, FC):
                round_up(fU[:, c, :], fq[:, 5:6], fu_rounded)
            act.wait_ge(fq_ready, 3)
            for c in range(FC):
                round_up(fG[:, c, :], fq[:, 7:8], fh_rounded)
            act.wait_ge(fq_ready, 4)
            for c in range(1, FC):
                round_up(fG[:, c, :], fq[:, 11:12], fo_rounded)

            a_mac = counter(act, "a_mac")
            a_s = counter(act, "a_s")
            a_t = counter(act, "a_t")
            a_x = counter(act, "a_x")
            a_f = counter(act, "a_f")
            a_nm = counter(act, "a_nm")
            a_u = counter(act, "a_u")
            act.wait_ge(fx_updated, B)
            act.sem_inc(s_free, SB)
            act.sem_inc(o_free, 2)
            act.sem_inc(u_kept, 1)
            act.wait_ge(ln_var, 3)
            nc.scalar.activation(rstd[:, :], mv[:, :, 1], ACT.Sqrt, bias=eps[:, :]).then_inc(ln_std, 1)
            act.wait_ge(c_loaded, 16 * 8)
            nc.scalar.activation(cBq[:, 1:2], cBq[:, 0:1], ACT.Copy, scale=SCALE_C)
            act.wait_ge(c_kv_done, 1)
            for i in range(2):
                half = slice(i * CR // 2, (i + 1) * CR // 2)
                nc.scalar.copy(kf[:, half], bank[i][:, 0:CR // 2]).then_inc(c_k_kept, 1)
                nc.scalar.copy(kp[:, 0, half], bank[i][:, 0:CR // 2]).then_inc(c_k_kept, 1)
            act.drain()

            def keep_queries(scale, bias, first=False):
                if not first:
                    act.wait_ge(fill_loaded, act.snap(a_f) * (16 * FILLS))
                act.reg_add(a_f, a_f, 1)
                wait_count(act, q_full, a_x)
                nc.scalar.activation(qf, bank[1][:, :], ACT.Identity, bias=bias, scale=scale)
                nc.scalar.activation(qp[:, 0, :], bank[1][:, :], ACT.Identity, bias=bias, scale=scale).then_inc(q_kept, 1)

            def keep_x():
                act.reg_add(a_x, a_x, 1)
                wait_count(act, xt_full, a_x)
                nc.scalar.copy(xT, bank[2][:, :]).then_inc(xt_kept, 1)

            def context_prepare(first=False):
                keep_x()
                keep_queries(SCALE_C, cBq[:, 1:2], first)

            def keep_maxima(first=False):
                if not first:
                    act.wait_ge(nm_loaded, act.snap(a_nm) * 16)
                act.reg_add(a_nm, a_nm, 1)
                wait_count(act, nmt_full, a_nm)
                nc.scalar.copy(nmS[0:3 * H, 0, :], bank[0][:, :].bitcast(BF16)[0:3 * H, 0:S]).then_inc(nms_full, 1)

            def attend(tq, tk):
                hp, banks, N, blocks, loops = shape_of(tq)

                def keep_output(c0, cp, plus):
                    act.wait_ge(av_done, act.snap(a_mac) + plus)
                    dst = Osb[:, cp:cp + 1, 0:N] if loops == 1 else Osb[:, bass.ds(act.snap(c0 + cp), 1), 0:N]
                    nc.scalar.copy(dst.rearrange("p c n -> p (c n)"), bank[4 + cp % 2][:, 0:N]).then_inc(o_free, 1)

                def one_pass(c0):
                    x = 0
                    for m in range(blocks * tk):
                        for i in range(banks):
                            act.wait_ge(s_full, act.snap(a_s) + (x + 1))
                            if i == 0:
                                act.wait_ge(av_done, act.snap(a_mac) + (m + 1))
                            nc.scalar.activation(PB[m % 2][:, i * hp * N:(i + 1) * hp * N], s_bank[x % SB][:, 0:hp * N], ACT.Exp)\
                                .then_inc(s_free, 1)
                            x += 1
                            if m and m % tk == 0 and i == min(2, banks - 1):
                                keep_output(c0, m // tk - 1, m + 2)
                    keep_output(c0, blocks - 1, blocks * tk + 2)
                    act.reg_add(a_s, a_s, x)
                    act.reg_add(a_mac, a_mac, blocks * tk)

                wait_count(act, t_full, a_t, 1)
                if loops == 1:
                    one_pass(0)
                else:
                    with act.Fori(0, loops, 1) as it:
                        one_pass(it * blocks)
                act.reg_add(a_t, a_t, tq)

            def keep_tokens():
                act.reg_add(a_u, a_u, 1)
                wait_count(act, u_full, a_u, 1)
                nc.scalar.copy(Usb, bank[6][:, :]).then_inc(u_kept, 1)

            for b in range(2):
                context_prepare(b == 0)
            keep_maxima(True)
            context_prepare()
            with act.Fori(0, B, 1) as b:
                attend(TB, 2)
                with act.If(b < B - 1):
                    keep_maxima()
                with act.If(b < B - 3):
                    context_prepare()
                keep_tokens()

            act.wait_ge(ln_var, 4)
            nc.scalar.activation(rstd[:, :], mv[:, :, 1], ACT.Sqrt, bias=eps[:, :]).then_inc(ln_std, 1)
            for b in range(B):
                act.wait_ge(rx_turned, b + 1)
                nc.scalar.copy(rXT[:, b * S:(b + 1) * S], bank[b][:, :]).then_inc(rx_kept, 1)
            act.wait_ge(r_shift, 1)
            nc.scalar.activation(pr, lg, ACT.Exp).then_inc(r_exp, 1)
            for b in range(B):
                act.wait_ge(r_wt, b + 1)
                nc.scalar.copy(wTs[b][0:E, :], bank[b][0:E, :]).then_inc(r_wt_kept, 1)
            act.wait_ge(d_loaded, 16 * 14)
            nc.scalar.activation(bqk[:, 0, :], bqk[:, 0, :], ACT.Copy, scale=SCALE_E)
            act.wait_ge(r_counts, 1)
            a_d = counter(act, "a_d")

            def expert_prepare(g):
                e = act.snap(act.value_load(order[0:1, bass.ds(g, 1)], min_val=0, max_val=NG - 1) % E)
                act.reg_add(a_d, a_d, 1)
                keep_x()
                keep_queries(SCALE_E, bqk[:, 0, bass.ds(e, 1)])
                wait_count(act, k_full, a_d)
                nc.scalar.activation(kf[:, 0:S], bank[2][:, :], ACT.Identity, bias=bqk[:, 1, bass.ds(e, 1)])
                nc.scalar.activation(kp[:, 0, 0:S], bank[2][:, :], ACT.Identity, bias=bqk[:, 1, bass.ds(e, 1)])\
                    .then_inc(k_kept, 1)

            act.drain()
            for g in range(2):
                expert_prepare(g)
            keep_maxima()
            expert_prepare(2)
            with act.Fori(0, NG, 1) as g:
                tc = act.value_load(cnti[0:1, bass.ds(g, 1)], min_val=0, max_val=TB)
                for v in range(1, TB + 1):
                    with act.If(tc == v):
                        attend(v, v)
                keep_maxima()
                with act.If(g < NG - 3):
                    expert_prepare((g + 3) % NG)
                keep_tokens()

        @block.vector
        def _(dve):
            def layer_norm_stats():
                for n in range(NT):
                    nc.vector.bn_stats(stats[:, n, :], X[:, n, :])
                dve.drain()
                for n in range(NT):
                    t = nc.vector.bn_aggr(mv[:, n, :], stats[:, n, :])
                t.then_inc(ln_var, 1)

            def normalise(dst, n):
                return nc.vector.tensor_scalar(dst, X[:, n, :], mv[:, n, 0:1], rstd[:, n:n + 1], ALU.subtract, ALU.mult)

            for b in range(B):
                dve.wait_ge(x_loaded[b], 16)
            layer_norm_stats()
            dve.wait_ge(ln_std, 1)
            nc.vector.reciprocal(rstd[:, :], rstd[:, :])
            dve.drain()

            def feed(b):
                p = b % 2
                if b >= 2:
                    dve.wait_ge(axt_done, b - 1)
                for i in range(TB):
                    t = normalise(aXn[p][:, i, :], b * TB + i)
                t.then_inc(axn_ready, 1)

            feed(0)
            dve.wait_ge(akv_done, 1)
            nc.vector.tensor_copy(aV[:, :, 0, :], bank[4][:, :].rearrange("p (b d) -> p b d", b=B)).then_inc(av_ready, 1)
            nc.vector.tensor_copy(aV[0:K1, :, 1, :], bank[5][0:K1, :].rearrange("p (b d) -> p b d", b=B))\
                .then_inc(av_ready, 1)
            feed(1)

            dve.wait_ge(w3_loaded, 48)
            blocks = W3.rearrange("p c (n i) -> p (c n) i", i=32)
            wmax_b = wmax.rearrange("p (n o) -> p n o", o=1).broadcast_to([P, 3 * FC * NBLK, 32])
            winv_b = winv.rearrange("p (n o) -> p n o", o=1).broadcast_to([P, 3 * FC * NBLK, 32])
            nc.vector.tensor_reduce(wmax, blocks, AX.X, ALU.max, apply_absolute_value=True)
            dve.drain()
            nc.vector.tensor_scalar(wmax, wmax, 1.0 / 7.0, 1e-12, ALU.mult, ALU.max)
            dve.drain()
            nc.vector.reciprocal(winv, wmax)
            dve.drain()
            nc.vector.tensor_tensor(blocks, blocks, winv_b, ALU.mult)
            dve.drain()
            nc.vector.tensor_scalar(W3, W3, ROUND, ROUND, ALU.add, ALU.subtract)
            dve.drain()
            nc.vector.tensor_tensor(blocks, blocks, wmax_b, ALU.mult).then_inc(w3_quant, 1)

            for b in range(B):
                p = b % 2
                dve.wait_ge(as_done, b + 1)
                for j in range(2):
                    nc.vector.tensor_reduce(aMax[:, b, 2 * j:2 * j + 2],
                                            bank[4 + j][:, :].rearrange("p (i k) -> p i k", i=2)[:, :, 0:K], AX.X, ALU.max)
                dve.drain()
                nc.vector.tensor_scalar(aMax[:, b, :], aMax[:, b, :], -SCALE_A, None, ALU.mult).then_inc(amax_ready, 1)
                if b + 2 < B:
                    feed(b + 2)
                dve.wait_ge(apt_done, b + 1)
                if b >= 2:
                    dve.wait_ge(ao_done, b - 1)
                nc.vector.tensor_copy(aPT[p][:, 0, :], bank[6][:, :]).then_inc(apt_ready, 1)
                nc.vector.tensor_copy(aPT[p][0:K1, 1, :], bank[7][0:K1, :]).then_inc(apt_ready, 1)
                nc.vector.reciprocal(aInv[:, b, :], aSum[:, b, :])
                dve.wait_ge(gates_ready, 1)
                dve.drain()
                nc.vector.tensor_scalar(aInv[:, b, :], aInv[:, b, :], gates[:, 0:1], None, ALU.mult)
                dve.drain()
                dve.wait_ge(ao_done, b + 1)
                for i in range(TB):
                    t = nc.vector.scalar_tensor_tensor(out=X[:, b * TB + i, :], in0=bank[p][:, i * D:(i + 1) * D],
                                                       scalar=aInv[:, b, i:i + 1], in1=X[:, b * TB + i, :],
                                                       op0=ALU.mult, op1=ALU.add)
                t.then_inc(ax_updated, 1)

            def quantiser(i):
                dve.wait_ge(fmax_all, i + 1)
                m = fmax[:, 16 + i:17 + i]
                if i == 4:
                    nc.vector.tensor_tensor(fq[:, 10:11], fq[:, 4:5], fq[:, 6:7], ALU.mult)
                    dve.drain()
                    nc.vector.tensor_tensor(m, m, fq[:, 10:11], ALU.mult)
                    dve.drain()
                nc.vector.tensor_scalar(fq[:, 2 * i:2 * i + 1], m, 1.0 / Q16, 1e-12, ALU.mult, ALU.max)
                dve.drain()
                t = nc.vector.reciprocal(fq[:, 2 * i + 1:2 * i + 2], fq[:, 2 * i:2 * i + 1])
                if i == 4:
                    dve.drain()
                    t = nc.vector.tensor_tensor(fq[:, 11:12], fq[:, 9:10], fq[:, 10:11], ALU.mult)
                if i:
                    t.then_inc(fq_ready, 1)
                dve.drain()

            def round_up(v, inverse):
                nc.vector.tensor_scalar(v, v, inverse, ROUND, ALU.mult, ALU.add)
                dve.drain()

            def rescale(v, scale):
                return nc.vector.tensor_scalar(v, v, ROUND, scale, ALU.subtract, ALU.mult)

            dve.drain()
            layer_norm_stats()
            dve.wait_ge(ln_std, 2)
            nc.vector.reciprocal(rstd[:, :], rstd[:, :])
            dve.drain()
            for n in range(NT):
                normalise(fXn[:, n, :], n)
            dve.drain()
            nc.vector.tensor_reduce(fmax[:, 0:1], fXn, AX.XY, ALU.max, apply_absolute_value=True).then_inc(fmax_part, 1)
            quantiser(0)
            for b in range(B):
                round_up(fXn[:, b * TB:(b + 1) * TB, :], fq[:, 1:2])
                rescale(fXn[:, b * TB:(b + 1) * TB, :], fq[:, 0:1]).then_inc(fxq_ready, 1)
            for n in range(2 * FC * B):
                dve.wait_ge(fmm_done, n + 1)
                nc.vector.tensor_reduce(fpart[:, n:n + 1], bank[n % 8][:, :], AX.X, ALU.max, apply_absolute_value=True)\
                    .then_inc(fmm_max, 1)
                if n % (FC * B) == FC * B - 1:
                    m = 1 + n // (FC * B)
                    dve.drain()
                    nc.vector.tensor_reduce(fmax[:, m:m + 1], fpart[:, n + 1 - FC * B:n + 1], AX.X, ALU.max).then_inc(fmax_part, 1)
            quantiser(1)
            dve.wait_ge(fmm_kept, 2 * FC * B)
            for c in range(FC):
                if c == 0:
                    round_up(fG[:, c, :], fq[:, 3:4])
                else:
                    dve.wait_ge(fg_rounded, c)
                rescale(fG[:, c, :], fq[:, 2:3]).then_inc(fgq_ready, 1)
            quantiser(2)
            round_up(fU[:, 0, :], fq[:, 5:6])
            nc.vector.tensor_scalar(fU[:, 0, :], fU[:, 0, :], ROUND, None, ALU.subtract)
            for c in range(FC):
                dve.wait_ge(fsig_ready, c + 1)
                nc.vector.tensor_scalar(fS[c], fS[c], ROUND, 65535.0, ALU.subtract, ALU.min)
                dve.drain()
                nc.vector.scalar_tensor_tensor(out=fG[:, c, :], in0=fS[c], scalar=1.0 / 65536.0, in1=fG[:, c, :],
                                               op0=ALU.mult, op1=ALU.mult)
                dve.drain()
                nc.vector.tensor_reduce(fmax[:, 8 + c:9 + c], fG[:, c, :], AX.X, ALU.max, apply_absolute_value=True)
            dve.drain()
            nc.vector.tensor_reduce(fmax[:, 3:4], fmax[:, 8:8 + FC], AX.X, ALU.max).then_inc(fmax_part, 1)
            for c in range(1, FC):
                dve.wait_ge(fu_rounded, c)
                nc.vector.tensor_scalar(fU[:, c, :], fU[:, c, :], ROUND, None, ALU.subtract)
            quantiser(3)
            for c in range(FC):
                dve.wait_ge(fh_rounded, c + 1)
                nc.vector.scalar_tensor_tensor(out=fG[:, c, :], in0=fG[:, c, :], scalar=ROUND, in1=fU[:, c, :],
                                               op0=ALU.subtract, op1=ALU.mult)
                dve.drain()
                nc.vector.tensor_reduce(fmax[:, 8 + c:9 + c], fG[:, c, :], AX.X, ALU.max, apply_absolute_value=True)
            dve.drain()
            nc.vector.tensor_reduce(fmax[:, 4:5], fmax[:, 8:8 + FC], AX.X, ALU.max).then_inc(fmax_part, 1)
            quantiser(4)
            for c in range(FC):
                if c == 0:
                    round_up(fG[:, c, :], fq[:, 11:12])
                else:
                    dve.wait_ge(fo_rounded, c)
                rescale(fG[:, c, :], fq[:, 8:9]).then_inc(fo_ready, 1)
            for b in range(B):
                dve.wait_ge(fd_done, b + 1)
                nc.vector.scalar_tensor_tensor(out=X[:, b * TB:(b + 1) * TB, :].rearrange("p n d -> p (n d)"),
                                               in0=bank[b][:, :], scalar=gates[:, 2:3],
                                               in1=X[:, b * TB:(b + 1) * TB, :].rearrange("p n d -> p (n d)"),
                                               op0=ALU.mult, op1=ALU.add).then_inc(fx_updated, 1)

            v_m = counter(dve, "v_m")
            v_mac = counter(dve, "v_mac")
            v_t = counter(dve, "v_t")
            v_x = counter(dve, "v_x")
            v_y = counter(dve, "v_y")
            v_mall = counter(dve, "v_mall")
            left = counter(dve, "v_left")
            unit = counter(dve, "v_unit")
            two = counter(dve, "v_two")
            at_m = counter(dve, "v_at")
            dve.sem_inc(m_free, 2)
            dve.sem_inc(t_free, 2)
            dve.sem_inc(x_added, 1)
            Vs = Vr.rearrange("p (s k w) -> p s k w", s=4, k=TB)
            Vh = Vr.rearrange("p (s k h w) -> p s k h w", s=4, k=TB, h=H)

            def max_start(units, pairs):
                dve.reg_mov(left, units)
                dve.reg_mov(two, pairs - 1)
                dve.reg_mov(unit, 0)
                dve.reg_mov(at_m, 0)
                nc.vector.memset(mrun, -1e30)
                dve.drain()

            def max_bank(c, wide):
                dve.wait_ge(m_full, dve.snap(v_m) + (c + 1))
                n = 1 if wide else 2
                at = dve.snap(at_m, min_val=0, max_val=TB * H - (H // 2 if wide else H))
                nc.vector.tensor_reduce(mrun[:, bass.ds(at + n * c, n)], bank[2 + c % 2][:, :].rearrange("p (j k) -> p j k", j=n),
                                        AX.X, ALU.max).then_inc(m_free, 1)
                if c == 7:
                    dve.reg_add(v_m, v_m, 8)
                    dve.reg_add(unit, unit, 1)
                    dve.reg_sub(left, left, 1)
                    u = dve.snap(unit, min_val=0, max_val=2 * TB)
                    w = dve.snap(two, min_val=0, max_val=1)
                    dve.reg_mov(at_m, (u >> w) * H + (u & w) * (H // 2))

            def max_rest():
                with dve.If(dve.snap(left) > 0):
                    with dve.If(dve.snap(two) > 0):
                        with dve.Fori(0, dve.snap(left), 1):
                            for c in range(8):
                                max_bank(c, True)
                    with dve.Else():
                        with dve.Fori(0, dve.snap(left), 1):
                            for c in range(8):
                                max_bank(c, False)
                    dve.nop()
                dve.nop()

            def max_end(first=False):
                if not first:
                    wait_count(dve, nmt_full, v_mall)
                dve.reg_add(v_mall, v_mall, 1)
                dve.drain()
                nc.vector.tensor_scalar(mall.rearrange("p q h -> p (q h)"), mrun, -1.0, None, ALU.mult)
                dve.drain()
                nc.vector.tensor_copy(nm[:, :, 0, :], mall)
                dve.drain()
                nc.vector.tensor_tensor(mres, mall, nm[:, :, 0, :], ALU.subtract)
                dve.drain()
                nc.vector.tensor_copy(nm[:, :, 1, :], mres)
                dve.drain()
                nc.vector.tensor_tensor(nm[:, :, 2, :], mres, nm[:, :, 1, :], ALU.subtract).then_inc(nm_split, 1)

            def attend(slot, tq, tk, modes):
                hp, banks, N, blocks, loops = shape_of(tq)

                def values(c0, c, plus):
                    dve.wait_ge(av_done, dve.snap(v_mac) + plus)
                    at = (c0 + c) * (4 * VW)
                    nc.vector.tensor_copy(V4[c % 2][:, 0:tk, :, :].rearrange("p k j w -> p k (j w)"),
                                          Vs[:, bass.ds(slot, 1), 0:tk, bass.ds(dve.snap(at) if loops > 1 else at, 4 * VW)]
                                          .rearrange("p s k w -> p (s k) w")).then_inc(v4_full, 1)

                def one_pass(c0):
                    values(c0, 0, 2)
                    values(c0, 1, 2)
                    steps = [(m, i) for m in range(blocks * tk) for i in range(banks)]
                    for x in range(0, len(steps), 8):
                        xs = range(x, min(x + 8, len(steps)))
                        if tq > 1:
                            with dve.If(dve.snap(left) > 0):
                                if len(modes) == 1:
                                    for y in xs:
                                        max_bank(y % 8, modes[0])
                                else:
                                    with dve.If(dve.snap(two) > 0):
                                        for y in xs:
                                            max_bank(y % 8, True)
                                    with dve.Else():
                                        for y in xs:
                                            max_bank(y % 8, False)
                                    dve.nop()
                        for y in xs:
                            m, i = steps[y]
                            if m and m % tk == 0 and i == min(2, banks - 1) and m // tk + 1 < blocks:
                                values(c0, m // tk + 1, 2 + m)
                    dve.reg_add(v_mac, v_mac, blocks * tk)

                if loops == 1:
                    one_pass(0)
                else:
                    with dve.Fori(0, loops, 1) as it:
                        one_pass(it * blocks)

            def normalise_out(tq, weight):
                dve.drain()
                for q in range(tq):
                    dve.reg_add(v_t, v_t, 1)
                    wait_count(dve, t_full, v_t, 1)
                    T = bank[6 + q % 2][:, :].rearrange("p (h w) -> p h w", h=H)
                    nc.vector.reciprocal(rinv[:, q, :], T[:, :, HD])
                    dve.drain()
                    if weight is not None:
                        nc.vector.tensor_scalar(rinv[:, q, :], rinv[:, q, :], tokw[:, bass.ds(dve.snap(weight + q), 1)], None, ALU.mult)
                        dve.drain()
                    nc.vector.tensor_tensor(ON[:, q, :].rearrange("p (h d) -> p h d", h=H), T[:, :, 0:HD],
                                            rinv[:, q, :].rearrange("p (h o) -> p h o", o=1).broadcast_to([P, H, HD]), ALU.mult)\
                        .then_inc(t_free, 1)

            def add_out(b, gate):
                dve.reg_add(v_y, v_y, 1)
                wait_count(dve, y_full, v_y)
                xb = X2[:, bass.ds(dve.snap(b * S), S)]
                nc.vector.scalar_tensor_tensor(out=xb, in0=bank[7][:, :], scalar=gate, in1=xb, op0=ALU.mult, op1=ALU.add)\
                    .then_inc(x_added, 1)

            def feed_context(b):
                if not (isinstance(b, int) and b == 0):
                    wait_count(dve, xt_full, v_x)
                dve.reg_add(v_x, v_x, 1)
                for i in range(TB):
                    if isinstance(b, int):
                        t = normalise(lXn[:, i, :], b * TB + i)
                    else:
                        n = dve.snap(b * TB + i)
                        t = nc.vector.tensor_scalar(lXn[:, i, :], X2[:, bass.ds(dve.snap(n * D), D)], mv2[:, bass.ds(dve.snap(n * 2), 1)],
                                                    rstd[:, bass.ds(n, 1)], ALU.subtract, ALU.mult)
                t.then_inc(xn_ready, 1)

            def split(v, p):
                nc.vector.tensor_tensor(v, v, p[:, 0, :], ALU.subtract)
                dve.drain()
                nc.vector.tensor_copy(p[:, 1, :], v)
                dve.drain()
                return nc.vector.tensor_tensor(p[:, 2, :], v, p[:, 1, :], ALU.subtract)

            def split_context(b):
                dve.wait_ge(q_kept, b + 1)
                split(qf, qp).then_inc(split_ready, 1)

            mv2 = mv[:, :, :].rearrange("p n c -> p (n c)")
            dve.drain()
            layer_norm_stats()
            dve.wait_ge(ln_std, 3)
            nc.vector.reciprocal(rstd[:, :], rstd[:, :])
            dve.drain()
            feed_context(0)
            dve.wait_ge(vr_zeroed, 1)
            dve.wait_ge(c_kv_done, 1)
            nc.vector.tensor_copy(Vh[:, :, 0, :, 0:HD], bank[2][:, :].rearrange("p (b h d) -> p b h d", b=B, h=H))\
                .then_inc(c_v_kept, 1)
            nc.vector.tensor_copy(Vh[0:K1, :, 1, :, 0:HD], bank[3][0:K1, :].rearrange("p (b h d) -> p b h d", b=B, h=H))\
                .then_inc(c_v_kept, 1)
            dve.wait_ge(c_k_kept, 4)
            split(kf, kp).then_inc(c_k_split, 1)
            feed_context(1)
            split_context(0)
            split_context(1)
            feed_context(2)
            dve.wait_ge(av_done, 2)
            max_start(TB, 1)
            max_rest()
            max_end(True)
            split_context(2)
            with dve.Fori(0, B, 1) as b:
                with dve.If(b < B - 1):
                    max_start(TB, 1)
                attend(b, TB, 2, (False,))
                max_rest()
                with dve.If(b < B - 1):
                    max_end()
                normalise_out(TB, None)
                with dve.If(b < B - 3):
                    feed_context((b + 3) % B)
                add_out(b, gates[:, 1:2])

            dve.drain()
            layer_norm_stats()
            dve.wait_ge(ln_std, 4)
            nc.vector.reciprocal(rstd[:, :], rstd[:, :])
            dve.drain()
            for n in range(NT):
                t = normalise(rXn[:, n, :], n)
            t.then_inc(rn_ready, 1)
            x_part = [xr[:, r * NT:(r + 1) * NT, :] for r in range(3)]
            dve.drain()
            nc.vector.tensor_copy(x_part[0], rXn)
            dve.wait_ge(rx_turned, B)
            dve.drain()
            nc.vector.tensor_tensor(rXn, rXn, x_part[0], ALU.subtract)
            dve.drain()
            nc.vector.tensor_copy(x_part[1], rXn)
            dve.wait_ge(d_loaded, 16 * 14)
            dve.wait_ge(r_logits, 1)

            def over_experts(v):
                return v.rearrange("p (n o) -> p n o", o=1).broadcast_to([P, NT, E])

            nc.vector.tensor_tensor(lg, bank[4][:, 0:NT * E].rearrange("p (n e) -> p n e", n=NT),
                                    rbb.rearrange("p (o e) -> p o e", o=1).broadcast_to([P, NT, E]), ALU.add)
            dve.drain()
            nc.vector.tensor_reduce(rsum, lg, AX.X, ALU.max)
            dve.drain()
            nc.vector.tensor_tensor(lg, lg, over_experts(rsum), ALU.subtract).then_inc(r_shift, 1)
            dve.wait_ge(d_consts, 5)
            dve.wait_ge(r_exp, 1)
            nc.vector.tensor_reduce(rsum, pr, AX.X, ALU.add)
            dve.drain()
            nc.vector.reciprocal(rsum, rsum)
            dve.drain()
            nc.vector.tensor_tensor(pr, pr, over_experts(rsum), ALU.mult)
            dve.drain()
            for d in range(1, E):
                nc.vector.tensor_tensor(cmp[:, :, 0:E - d], pr[:, :, d:E], pr[:, :, 0:E - d], ALU.is_gt)
                dve.drain()
                nc.vector.tensor_tensor(rank[:, :, 0:E - d], rank[:, :, 0:E - d], cmp[:, :, 0:E - d], ALU.add)
                dve.drain()
                nc.vector.tensor_tensor(rank[:, :, d:E], rank[:, :, d:E], cmp[:, :, 0:E - d], ALU.subtract)
                dve.drain()
            nc.vector.tensor_scalar(memb.rearrange("p t (b e) -> p b t e", b=B), rank.rearrange("p (b t) e -> p b t e", b=B),
                                    2.0, None, ALU.is_lt)
            nc.vector.scalar_tensor_tensor(out=wgt, in0=rank, scalar=2.0, in1=pr, op0=ALU.is_lt, op1=ALU.mult)\
                .then_inc(r_memb, 1)
            dve.drain()
            parts = info.rearrange("p (n e) c -> p n e c", n=NT)
            nc.vector.tensor_copy(parts[:, :, :, 2], wgt)
            dve.drain()
            nc.vector.tensor_tensor(pr, wgt, parts[:, :, :, 2], ALU.subtract)
            dve.drain()
            nc.vector.tensor_copy(parts[:, :, :, 3], pr)
            dve.drain()
            nc.vector.tensor_tensor(parts[:, :, :, 4], pr, parts[:, :, :, 3], ALU.subtract).then_inc(r_info, 1)
            dve.wait_ge(r_pos, 1)
            nc.vector.scalar_tensor_tensor(out=posm, in0=bank[5][:, 0:TB * NG].rearrange("p (t g) -> p t g", t=TB), scalar=1.0,
                                           in1=memb, op0=ALU.add, op1=ALU.mult)
            dve.drain()
            nc.vector.tensor_scalar(posm, posm, 1.0, None, ALU.subtract)
            dve.wait_ge(r_cnt, 1)
            nc.vector.memset(cnti[:, :], 0)
            nc.vector.memset(order[:, :], 0)
            nc.vector.tensor_scalar(cntr[0:1, 0, :], bank[6][0:1, 0:NG], float(P), 1.0, ALU.is_gt, ALU.add)
            dve.drain()
            for i in range(2, TB):
                nc.vector.scalar_tensor_tensor(out=cntr[0:1, (i - 1) % 2, :], in0=bank[6][0:1, 0:NG],
                                               scalar=float(i * P), in1=cntr[0:1, i % 2, :], op0=ALU.is_gt, op1=ALU.add)
                dve.drain()
            nc.vector.tensor_scalar(cntr[0:1, (TB - 1) % 2, :], bank[6][0:1, 0:NG], 1.0, None, ALU.max)

            def by_row(v):
                return v.rearrange("p (a o) -> p a o", o=1).broadcast_to([1, NG, NG])

            def by_column(v):
                return v.rearrange("p (o a) -> p o a", o=1).broadcast_to([1, NG, NG])

            nc.vector.scalar_tensor_tensor(out=key, in0=bank[6][0:1, 0:NG], scalar=float(NG), in1=iota[0:1, 0:NG],
                                           op0=ALU.mult, op1=ALU.add)
            dve.drain()
            nc.vector.tensor_tensor(pair, by_row(key), by_column(key), ALU.is_gt)
            dve.drain()
            nc.vector.tensor_reduce(rk, pair, AX.X, ALU.add)
            dve.drain()
            nc.vector.tensor_tensor(pair, by_row(iota[0:1, 0:NG]), by_column(rk), ALU.is_equal)
            dve.drain()
            for v, placed in ((iota[0:1, 0:NG], ord_f), (cntr[0:1, TB % 2, :], til_f),
                              (cntr[0:1, (TB - 1) % 2, :], cnt[0:1, :])):
                nc.vector.tensor_tensor(pair_v, pair, by_column(v), ALU.mult)
                dve.drain()
                nc.vector.tensor_reduce(placed, pair_v, AX.X, ALU.add)
                dve.drain()
            nc.vector.tensor_copy(order[:, 0:NG], ord_f)
            nc.vector.tensor_copy(cnti[:, 0:NG], til_f).then_inc(r_counts, 1)
            nc.vector.tensor_tensor(x_part[2], rXn, x_part[1], ALU.subtract).then_inc(xr_ready, 1)

            def add_biases():
                for b in range(B):
                    dve.wait_ge(r_bias_full, b + 1)
                    xb = X2[:, b * S:(b + 1) * S]
                    nc.vector.scalar_tensor_tensor(out=xb, in0=bank[6 + b % 2][:, :], scalar=gates[:, 3:4], in1=xb,
                                                   op0=ALU.mult, op1=ALU.add).then_inc(r_bias_added, 1)

            def split_expert(g):
                dve.wait_ge(q_kept, B + g + 1)
                split(qf, qp)
                dve.wait_ge(k_kept, g + 1)
                split(kf[:, 0:S], kp[:, :, 0:S]).then_inc(split_ready, 1)
                dve.drain()

            v_d = counter(dve, "v_d")

            def group_at(g):
                return dve.value_load(order[0:1, bass.ds(g, 1)], min_val=0, max_val=NG - 1)

            def one_hot(g):
                which = group_at(g)
                for t in range(TB):
                    h = nc.vector.tensor_scalar(G[:, t, :], iota16, posm[:, t, bass.ds(which, 1)], None, ALU.is_equal)
                h.then_inc(g_built, 1)

            def one_hot_back(slot, tq):
                for t in range(tq):
                    h = nc.vector.tensor_scalar(GT[:, t, :], iota16, tokw[:, bass.ds(dve.snap(slot * (2 * TB) + t), 1)], None,
                                                ALU.is_equal)
                h.then_inc(gt_built, 1)

            def expert_prepare(g):
                which = group_at(g)
                dve.reg_add(v_d, v_d, 1)
                wait_count(dve, info_full, v_d)
                nc.vector.tensor_copy(isb, bank[3][:, 0:TB * 8].rearrange("p (t c) -> p t c", t=TB)).then_inc(info_kept, 1)
                dve.drain()
                slot = dve.snap(g % 4)
                at = dve.snap(slot * 8)
                at4 = dve.snap(slot * 8 + TB)
                nc.vector.scalar_tensor_tensor(out=tokw[:, bass.ds(at, TB)], in0=isb[:, :, 1], scalar=float(P), in1=isb[:, :, 0],
                                               op0=ALU.mult, op1=ALU.add)
                nc.vector.tensor_tensor(isb[:, :, 5], isb[:, :, 2], isb[:, :, 3], ALU.add)
                dve.drain()
                nc.vector.tensor_tensor(tokw[:, bass.ds(at4, TB)], isb[:, :, 5], isb[:, :, 4], ALU.add)
                dve.wait_ge(fill_loaded, dve.snap((dve.snap(v_d) + (B - 1)) * (16 * FILLS)))
                nc.vector.tensor_scalar(mrow[0:1, 1, :], iota[0:1, :], cnt[0:1, bass.ds(g, 1)], NEG, ALU.is_ge, ALU.mult)\
                    .then_inc(mask_ready, 1)
                wait_count(dve, v_full, v_d)
                nc.vector.tensor_tensor(Vh[:, bass.ds(slot, 1), :, :, 0:HD].rearrange("p s k h d -> p (s k) h d"),
                                        bank[3][:, :].rearrange("p (k h d) -> p k h d", k=TB, h=H),
                                        bvb[:, bass.ds(dve.snap(which % E), 1), :].rearrange("p e (h d) -> p e h d", h=H)
                                        .broadcast_to([P, TB, H, HD]), ALU.add).then_inc(v_kept, 1)
                dve.drain()

            def tiles(g):
                return dve.value_load(cnti[0:1, bass.ds(g, 1)], min_val=0, max_val=TB)

            dve.drain()
            one_hot(0)
            for g in range(2):
                expert_prepare(g)
                split_expert(g)
                one_hot(g + 1)
                if g == 0:
                    add_biases()
            tn = tiles(0)
            max_start(tn * ((tn + 1) >> 1), (tn + 1) >> 1)
            max_rest()
            max_end()
            expert_prepare(2)
            split_expert(2)
            one_hot(3)
            tc = counter(dve, "v_tc")
            tnext = counter(dve, "v_tnext")
            dve.reg_mov(tc, tn)
            t1 = tiles(1)
            dve.reg_mov(tnext, t1)
            max_start(t1 * ((t1 + 1) >> 1), (t1 + 1) >> 1)
            with dve.Fori(0, NG, 1) as g:
                slot = dve.snap(g % 4)
                weight = dve.snap(slot * 8 + TB)
                for v in range(1, TB + 1):
                    with dve.If(dve.snap(tc) == v):
                        attend(slot, v, v, (True,) if v > 2 else (True, False))
                        max_rest()
                        max_end()
                        normalise_out(v, weight)
                        one_hot_back(slot, v)
                t2 = tiles(g + 2)
                max_start(t2 * ((t2 + 1) >> 1), (t2 + 1) >> 1)
                dve.reg_mov(tc, tnext)
                dve.reg_mov(tnext, t2)
                batch = dve.snap(group_at(g) // E)
                with dve.If(g < NG - 3):
                    expert_prepare((g + 3) % NG)
                with dve.If(g < NG - 4):
                    one_hot((g + 4) % NG)
                add_out(batch, gates[:, 3:4])


_INS = ['x', 'ctx_768', 'g_xattn', 'g_ffn', 'L0_xattn_Wq', 'L0_xattn_bq', 'L0_xattn_Wk', 'L0_xattn_bk', 'L0_xattn_Wv',
        'L0_xattn_bv', 'L0_ffn_w_gate', 'L0_ffn_w_up', 'L0_ffn_w_down', 'L1_xattn_w_q', 'L1_xattn_b_q', 'L1_xattn_w_k',
        'L1_xattn_b_k', 'L1_xattn_w_v', 'L1_xattn_b_v', 'L1_xattn_w_o', 'L1_xattn_b_o', 'L1_ffn_router_w',
        'L1_ffn_router_b', 'L1_ffn_wq', 'L1_ffn_bq', 'L1_ffn_wk', 'L1_ffn_bk', 'L1_ffn_wv', 'L1_ffn_bv', 'L1_ffn_wo',
        'L1_ffn_bo']


def kernel(**inputs):
    import numpy as _np
    import concourse.bacc as _bacc
    from concourse.bass_utils import run_bass_kernel_spmd as _run

    nc = _bacc.Bacc("TRN2", target_bir_lowering=False, num_devices=1)
    arrays, args = {}, []
    for name in _INS:
        a = _np.ascontiguousarray(inputs[name])
        arrays[f"in_{name}_dram"] = a
        args.append(nc.dram_tensor(f"in_{name}_dram", a.shape, mybir.dt.from_np(a.dtype), kind="ExternalInput").ap())
    args.append(nc.dram_tensor("out_0_dram", inputs["x"].shape, F32, kind="ExternalOutput").ap())
    build(nc, *args)
    r = _run(nc, [arrays], core_ids=[0])
    return r.results[0]["out_0_dram"]
```
